# Optimizing a Trainium2 kernel written in Bass

```python
import numpy as np
import jax
import jax.numpy as jnp

def _softmax(x, axis=-1):
    return jax.nn.softmax(x, axis=axis)

def _gelu(x):
    return jax.nn.gelu(x, approximate=True)

def _silu(x):
    return jax.nn.silu(x)

def _sigmoid(x):
    return jax.nn.sigmoid(x)

def _layernorm(x, axis=-1, eps=1e-05):
    m = jnp.mean(x, axis=axis, keepdims=True)
    v = jnp.var(x, axis=axis, keepdims=True)
    return (x - m) / jnp.sqrt(v + eps)

def _scatter_add(tgt, idx, src, axis=0):
    return tgt.at[idx].add(src)

def _segment_sum(src, seg, n):
    return jax.ops.segment_sum(src, seg, n)
kernel_name = 'mk_recurrent_d1_jaxref_r8_971093'

def setup_inputs(seed: int=0):
    np.random.seed(seed)
    _w = jnp.asarray

    def _L0_attn_setup():
        import jax, jax.numpy as jnp
        import numpy as np
        B, C, D, H = (2, 256, 128, 16)
        HE = D // H
        key = jax.random.key(seed)
        k1, k2, k3, k4, k5 = jax.random.split(key, 5)
        s = 0.02
        return {'x': jax.random.normal(k1, (B, C, D), dtype=jnp.float32), 'Wqkv': jax.random.normal(k2, (HE, 3 * HE), dtype=jnp.float32) * s, 'bqkv': jax.random.normal(k3, (3 * HE,), dtype=jnp.float32) * s, 'Wr': jax.random.normal(k4, (D, D), dtype=jnp.float32) * s, 'br': jax.random.normal(k5, (D,), dtype=jnp.float32) * s}
    _L0_attn_in = _L0_attn_setup()

    def _L0_ffn_setup():
        import jax, jax.numpy as jnp
        import numpy as np
        FP8_MAX = 448.0
        key = jax.random.key(seed)
        k_x, k_w, k_b = jax.random.split(key, 3)
        B, S, IN, OUT = (4, 1024, 128, 128)
        x = jax.random.normal(k_x, (B, S, IN), dtype=jnp.float32)
        w_fp32 = jax.random.normal(k_w, (OUT, IN), dtype=jnp.float32)
        weight_fp8 = w_fp32.astype(jnp.float8_e4m3fn).astype(jnp.float32)
        bias = jax.random.normal(k_b, (OUT,), dtype=jnp.float32)
        input_scale = jnp.ones((1,), dtype=jnp.float32)
        weight_scale = jnp.ones((1,), dtype=jnp.float32)
        return {'x': x, 'weight_fp8': weight_fp8, 'bias': bias, 'input_scale': input_scale, 'weight_scale': weight_scale}
    _L0_ffn_in = _L0_ffn_setup()
    _d = {'L0_attn_x': _L0_attn_in['x'], 'L0_attn_Wqkv': _L0_attn_in['Wqkv'], 'L0_attn_bqkv': _L0_attn_in['bqkv'], 'L0_attn_Wr': _L0_attn_in['Wr'], 'L0_attn_br': _L0_attn_in['br'], 'L0_ffn_weight_fp8': _L0_ffn_in['weight_fp8'], 'L0_ffn_bias': _L0_ffn_in['bias'], 'L0_ffn_input_scale': _L0_ffn_in['input_scale'], 'L0_ffn_weight_scale': _L0_ffn_in['weight_scale']}
    _x0 = _d['L0_attn_x']
    _d['L0_attn_x'] = jax.random.normal(jax.random.fold_in(jax.random.key(seed), 1), (4, 1024, 128), dtype=_x0.dtype)
    del _x0
    return _d

def reference(L0_attn_x, L0_attn_Wqkv, L0_attn_bqkv, L0_attn_Wr, L0_attn_br, L0_ffn_weight_fp8, L0_ffn_bias, L0_ffn_input_scale, L0_ffn_weight_scale):

    def _L0_attn_ref(x, Wqkv, bqkv, Wr, br):
        import jax, jax.numpy as jnp
        import numpy as np
        B, C, D, H = (2, 256, 128, 16)
        HE = D // H
        b, c, d = x.shape
        h, he = (H, HE)
        xh = x.reshape(b, c, h, he).transpose(0, 2, 1, 3)
        qkv = jnp.einsum('bhce,ef->bhcf', xh, Wqkv) + bqkv
        q, k, v = jnp.split(qkv, 3, axis=-1)
        att = jnp.einsum('bhqe,bhke->bhqk', q, k) / jnp.sqrt(jnp.float32(he))
        mask = jnp.tril(jnp.ones((c, c), dtype=att.dtype), k=-1)
        att = jax.nn.softmax(att * mask, axis=-1)
        out = jnp.einsum('bhqk,bhke->bhqe', att, v)
        out = out.transpose(0, 2, 1, 3).reshape(b, c, d)
        out = out @ Wr + br
        return out

    def _L0_ffn_ref(x, weight_fp8, bias, input_scale, weight_scale):
        import jax, jax.numpy as jnp
        import numpy as np
        FP8_MAX = 448.0
        x_q = jnp.clip(x / input_scale, -FP8_MAX, FP8_MAX)
        x_dq = x_q.astype(jnp.float8_e4m3fn).astype(x.dtype) * input_scale
        w_dq = weight_fp8 * weight_scale
        out = jnp.einsum('bsi,oi->bso', x_dq, w_dq) + bias
        return out
    x = L0_attn_x
    xn = _layernorm(x, axis=-1)
    s = _L0_attn_ref(xn, L0_attn_Wqkv, L0_attn_bqkv, L0_attn_Wr, L0_attn_br)
    g = _silu(_L0_ffn_ref(xn, L0_ffn_weight_fp8, L0_ffn_bias, L0_ffn_input_scale, L0_ffn_weight_scale))
    x = x + s * g
    return x

_drawn_inputs = setup_inputs


def setup_inputs(seed=0):
    import zlib

    import numpy as np

    out = dict(_drawn_inputs(seed))
    spreads = {}
    factors = {'L0_attn_Wqkv': 8.0, 'L0_ffn_bias': 4.136}
    for name, (base, spread) in spreads.items():
        noise = np.random.default_rng([zlib.crc32(name.encode()), seed]).standard_normal(out[name].shape)
        drawn = base * np.exp(spread * noise) if base else spread * noise
        out[name] = jnp.asarray(drawn.astype(out[name].dtype))
    for name, factor in factors.items():
        out[name] = (out[name] * factor).astype(out[name].dtype)
    return out
```

```python
from contextlib import ExitStack

import numpy as np

import concourse.bass as bass
from concourse import mybir

F32 = mybir.dt.float32
BF16 = mybir.dt.bfloat16
FP8 = mybir.dt.float8e4
I32 = mybir.dt.int32
ALU = mybir.AluOpType
ACT = mybir.ActivationFunctionType
AX = mybir.AxisListType

P = 128
B, C, D, H = 4, 1024, 128, 16
HE = D // H
TOK = B * C
NBLK = TOK // P
CB = C // P
G = 4
NG = H // G
STEPS = B * NG
PT = 512
PB = PT // P
PIECES = TOK // PT
NP3 = 3
ROWS = NP3 * NP3 * HE
MROW = 96
VC = HE + 1
SCALE = float(1.0 / np.sqrt(np.float32(HE)))
EPS = 1e-5
FP8_MAX = 448.0
FINE = 16.0



def score_units():
    units = []
    for half in (1, 0):
        blocks = range(half * 4, half * 4 + 4)
        units += [(True, i, (0, 1, 2, 3), i, 1) for i in blocks]
        for i in reversed(blocks):
            if i >= 4:
                units += [(False, i, (h,), 0, 4) for h in range(G)]
            rest, first = i % 4, i - i % 4
            if rest == 3:
                units += [(False, i, (h,), first, 3) for h in range(G)]
            elif rest:
                per = 4 // rest
                units += [(False, i, tuple(range(h, h + per)), first, rest) for h in range(0, G, per)]
    return units


def attend_units():
    units = []
    for half in (1, 0):
        for kb in range(4 * half + 4):
            q0 = max(half * PT, kb * P)
            n = (half + 1) * PT - q0
            for heads in (((0, 1), (2, 3)) if n > PT // 2 else ((0, 1, 2, 3),)):
                units.append((half, kb, heads, q0, n))
    return units


SU = score_units()
AU = attend_units()
NSU, NAU = len(SU), len(AU)
NSD = sum(u[0] for u in SU)
NSR = NSU - NSD
HALF1 = max(n for n, u in enumerate(SU) if u[1] >= 4) + 1
PV = [(half, kb) for half in (1, 0) for kb in range(4 * half + 4)]
NPV = len(PV)
MASKED = [n for n, (half, kb, _, q0, _) in enumerate(AU) if q0 == kb * P]
NMASK = len(MASKED)
RING = 5
LAG = 2


def step_order():
    order, s, m = [], 0, 0
    last_of = [max(n for n, u in enumerate(AU) if (u[0], u[1]) == pv) for pv in PV]
    for n in range(NAU + LAG + 1):
        if n < NAU:
            order.append(("AU", n))
        if n == 0:
            order.append(("MAX", 0, 0))
        if n == 3:
            order.append(("ROWS", 0, 0))
        upto = -(-HALF1 * min(n + 1, 14) // 14) if n < 14 else min(NSU, HALF1 + 2 * (n - 13))
        while s < upto:
            order.append(("SU", s))
            s += 1
            if s == HALF1:
                order.append(("MAX", 1, 1))
        while m < NPV and last_of[m] + LAG <= n:
            order.append(("PV", m))
            m += 1
            if m == NPV or PV[m][0] != PV[m - 1][0]:
                order.append(("OUT", PV[m - 1][0]))
        if n == 18:
            order.append(("ROWS", 1, 1))
    assert s == NSU and m == NPV
    return order


ORDER = step_order()


def program(nc, x, wqkv, bqkv, wr, br, wffn, bffn, iscale, wscale, out):
    ctx = ExitStack()
    with ctx:
        def sb(name, shape, dt=F32):
            return ctx.enter_context(nc.sbuf_tensor(name, shape, dt))

        def ps(name, shape, dt=F32):
            return ctx.enter_context(nc.psum_tensor(name, shape, dt))

        sems = {}

        def sem(name):
            sems[name] = ctx.enter_context(nc.semaphore(name))
            return sems[name]

        split_dram = nc.dram_tensor("split_dram", (2, NP3, P, TOK), BF16, kind="Internal").ap()
        x_all = sb("x_all", [P, NBLK, D])
        gate = sb("gate", [P, NBLK, D])
        v_all = sb("v_all", [P, NBLK, H, VC])
        num = sb("num", [P, NBLK, H, VC])
        q_op = sb("q_op", [P, 2, G, C], BF16)
        k_op = sb("k_op", [P, 2, G, C], BF16)
        v_op = sb("v_op", [P, 2, CB, G, 32])
        probs = sb("probs", [P, RING, 2 * PT])
        diag = sb("diag", [P, 2, 2, G, P])
        ident = sb("ident", [P, P])
        identb = sb("identb", [P, P], BF16)
        wrep = sb("wrep", [P, 3 * HE])
        wbd = sb("wbd", [P, 3, P])
        wbd_half = sb("wbd_half", [P, 3, P])
        bqk = sb("bqk", [P, 2])
        bv = sb("bv", [P, P])
        wr_sb = sb("wr_sb", [P, D])
        br_sb = sb("br_sb", [P, D])
        wf_raw = sb("wf_raw", [P, D])
        wf_dq = sb("wf_dq", [P, D])
        wf_t = sb("wf_t", [P, D])
        bf_sb = sb("bf_sb", [P, D])
        isc = sb("isc", [P, 1])
        risc = sb("risc", [P, 1])
        wsc = sb("wsc", [P, 1])
        stats = sb("stats", [P, NBLK, 6])
        mean2 = sb("mean2", [P, NBLK])
        mean = sb("mean", [P, NBLK])
        dev = sb("dev", [P, NBLK])
        dev2 = sb("dev2", [P, NBLK])
        m2 = sb("m2", [P, NBLK])
        var = sb("var", [P, NBLK])
        vareps = sb("vareps", [P, NBLK])
        std = sb("std", [P, NBLK])
        rstd = sb("rstd", [P, NBLK])
        count_i = sb("count_i", [P, CB], I32)
        count = sb("count", [P, CB])
        xn = sb("xn", [P, PB, D])
        xn_t = sb("xn_t", [P, PT])
        qk_f = sb("qk_f", [P, 2, PT])
        qk_r = sb("qk_r", [P, 2, PT])
        qk_p = sb("qk_p", [P, 2, NP3, PT], BF16)
        v_p = sb("v_p", [P, PB, D])
        suf_t = sb("suf_t", [P, PT])
        carry = sb("carry", [P, PIECES + B])
        xs = sb("xs", [P, PT])
        xs_half = sb("xs_half", [P, PT])
        x_fine = sb("x_fine", [P, PT], FP8)
        x_pos = sb("x_pos", [P, PT], FP8)
        x_neg = sb("x_neg", [P, PT], FP8)
        x_far = sb("x_far", [P, PT])
        x_q = sb("x_q", [P, PT])
        x_dq = sb("x_dq", [P, PT])
        z = sb("z", [P, PB, D])
        th = sb("th", [P, PB, D])
        sig = sb("sig", [P, PB, D])
        tops = sb("tops", [P, 2, 4, G, 3])
        top = sb("top", [P, 2, 4, G])
        e0 = sb("e0", [P, 2, 2, 4, G])
        top_r = sb("top_r", [P, 2, 4, G])
        top_p = sb("top_p", [P, 2, 4, NP3, G], BF16)
        top_t = sb("top_t", [NP3 * G, 2, PT], BF16)
        sums_t = sb("sums_t", [P, 2, PT])
        scaled = sb("scaled", [P, 2, 4, G, VC])
        rden = sb("rden", [P, PB, H])
        o_p = sb("o_p", [P, PB, D])
        o_t = sb("o_t", [P, PT])
        y1 = sb("y1", [P, PB, D])
        y2 = sb("y2", [P, PB, D])
        y3 = sb("y3", [P, PB, D])

        st_ps = ps("st_ps", [P, 2, 2, PT])
        s_ps = ps("s_ps", [P, 2, PT])
        pv_ps = ps("pv_ps", [P, PT])
        mix_ps = ps("mix_ps", [P, PT])
        mixb_ps = mix_ps[:, :].bitcast(BF16)

        for name in """waited x_loaded0 x_loaded1 x_loaded2 x_loaded3 weights_loaded wrep_loaded
                stats_done mean_done norm_ready sqrt_done setup_dve
                pool_const rows_set wbd_ready wf_scaled wf_full wf_ready
                xn_ready xt_full xt_copied qk_full qk_hi qk_float qk_res qk_mid qk_low split_stored
                v_full v_done v_copied vt_full scanned carry_done suf_full suf_done
                xs_done half_done fine_done pos_done neg_done far_done xq_done xdq_done
                ffn_full z_done th_done sig_done gate_done
                q_loaded s_full diag_copied diag_masked diag_reduced s_reduced
                top_ready e0_ready hi_ready res_ready mid_ready low_ready rows_full rows_copied rows_loaded
                v_op_ready st_full exp_done masked pv_done sums_copied sums_full scaled_done num_done
                den_inverted o_done ot_full ot_copied y_full y1_done y2_done y3_done stored""".split():
            sem(name)
        S = sems

        block = ctx.enter_context(nc.Block())

        def wait_apart(engine, semaphore, value):
            engine.wait_ge(semaphore, value)
            engine.sem_inc(S["waited"], 1)

        def piece_block(p):
            return 8 * (p // 2) + 4 * (1 - p % 2)

        def piece_carry(p):
            return p + p // 2

        def step_batch(u):
            return u // 2

        def step_head(u, par):
            return 8 * (u % 2) + 4 * par

        @block.sync
        def _(sp):
            x_v = x.rearrange("b (n p) d -> p (b n) d", p=P)
            sp.dma_start(wrep[:, :], wqkv.rearrange("(a e) f -> a e f", a=1).to_broadcast([H, HE, 3 * HE]))\
                .then_inc(S["wrep_loaded"], 16)
            for b in range(B):
                sp.dma_start(x_all[:, CB * b:CB * (b + 1), :], x_v[:, CB * b:CB * (b + 1), :])\
                    .then_inc(S[f"x_loaded{b}"], 16)

            def store_split(p):
                tok = P * piece_block(p)
                for side in range(2):
                    wait_apart(sp, S["qk_low"], 2 * p + side + 1)
                    sp.dma_start(split_dram[side, :, :, bass.ds(tok, PT)].rearrange("a p t -> p a t"),
                                 qk_p[:, side, :, :]).then_inc(S["split_stored"], 16)

            store_split(0)
            with sp.Fori(1, PIECES) as p:
                store_split(p)
            sp.wait_ge(S["split_stored"], 32 * PIECES)

            def load_operands(u, par, first=False):
                tok, row = C * step_batch(u), HE * step_head(u, par)
                t = 2 * u + par
                if not first:
                    wait_apart(sp, S["st_full"], NAU * (t - 1))
                    wait_apart(sp, S["s_full"], NSU * (t - 1))
                for j in range(G):
                    for a in range(NP3):
                        rows = slice(NP3 * HE * a, NP3 * HE * (a + 1))
                        q_a = split_dram[0, a:a + 1, bass.ds(row + HE * j, HE), bass.ds(tok, C)]
                        sp.dma_start(q_op[rows, par, j, :],
                                     q_a.rearrange("a f t -> f a t").to_broadcast([HE, NP3, C]))\
                            .then_inc(S["q_loaded"], 16)
                        k_b = split_dram[1, :, bass.ds(row + HE * j, HE), bass.ds(tok, C)]
                        sp.dma_start(k_op[rows, par, j, :], k_b.rearrange("b f t -> f b t"))\
                            .then_inc(S["q_loaded"], 16)

            def load_rows(par, half, t):
                sp.wait_ge(S["rows_copied"], 2 * t + (1 if half else 2))
                sp.dma_start(q_op[MROW:MROW + NP3, par, :, half * PT:(half + 1) * PT], top_t[:, half, :])\
                    .then_inc(S["rows_loaded"], 16)

            sp.wait_ge(S["pool_const"], 4)
            load_operands(0, 0, True)
            load_rows(0, 1, 0)
            load_operands(0, 1, True)

            def step(u, par, last=False, load=True):
                t = 2 * u + par
                load_rows(par, 0, t)
                if not last:
                    load_rows(1 - par, 1, t + 1)
                if load:
                    load_operands(u + 1, par)

            step(0, 0)
            step(0, 1)
            with sp.Fori(1, STEPS // 2 - 1) as u:
                step(u, 0)
                step(u, 1)
            step(STEPS // 2 - 1, 0, load=False)
            step(STEPS // 2 - 1, 1, last=True, load=False)

            out_v = out.rearrange("b (n p) d -> p (b n) d", p=P)

            def store(p):
                wait_apart(sp, S["y3_done"], p + 1)
                sp.dma_start(out_v[:, bass.ds(piece_block(p), PB), :], y3[:, :, :]).then_inc(S["stored"], 16)

            store(0)
            with sp.Fori(1, PIECES) as p:
                store(p)
            sp.wait_ge(S["stored"], 16 * PIECES)

        @block.scalar
        def _(act):
            for dst, src in (
                (bqk[:, 0:1], bqkv[0:HE].rearrange("(a e f) -> a e f", a=1, f=1).to_broadcast([H, HE, 1])),
                (bqk[:, 1:2], bqkv[HE:2 * HE].rearrange("(a e f) -> a e f", a=1, f=1).to_broadcast([H, HE, 1])),
                (bv[:, :], bqkv[2 * HE:].rearrange("(a b e) -> a b e", a=1, b=1).to_broadcast([P, H, HE])),
                (wr_sb[:, :], wr),
                (br_sb[:, :], br.rearrange("(a d) -> a d", a=1).to_broadcast([P, D])),
                (wf_raw[:, :], wffn),
                (bf_sb[:, :], bffn.rearrange("(a d) -> a d", a=1).to_broadcast([P, D])),
                (isc[:, :], iscale.rearrange("(a d) -> a d", a=1).to_broadcast([P, 1])),
                (wsc[:, :], wscale.rearrange("(a d) -> a d", a=1).to_broadcast([P, 1])),
            ):
                act.dma_start(dst, src).then_inc(S["weights_loaded"], 16)

            act.wait_ge(S["norm_ready"], 1)
            act.activation(std[:, :], vareps[:, :], ACT.Sqrt).then_inc(S["sqrt_done"], 1)
            act.wait_ge(S["wf_full"], 1)
            act.activation(wf_t[:, :], mix_ps[:, 0:P], ACT.Copy).then_inc(S["wf_ready"], 1)
            act.wait_ge(S["weights_loaded"], 144)

            def prepare(p, first=False):
                act.wait_ge(S["xt_full"], p + 1)
                if not first:
                    act.wait_ge(S["ffn_full"], p)
                    act.wait_ge(S["xs_done"], p)
                act.activation(xn_t[:, :], mix_ps[:, :], ACT.Copy).then_inc(S["xt_copied"], 1)
                for side in range(2):
                    act.wait_ge(S["qk_full"], 2 * p + side + 1)
                    if not first:
                        act.wait_ge(S["split_stored"], 32 * p)
                    act.activation(qk_p[:, side, 0, :], mix_ps[:, :], ACT.Identity,
                                   bias=bqk[:, side:side + 1]).then_inc(S["qk_hi"], 1)
                act.wait_ge(S["v_done"], p + 1)
                act.activation(v_all[:, bass.ds(piece_block(p), PB), :, 0:HE],
                               v_p[:, :, :].rearrange("p n (h e) -> p n h e", e=HE), ACT.Copy)\
                    .then_inc(S["v_copied"], 1)
                act.wait_ge(S["suf_full"], p + 1)
                act.activation(num[:, bass.ds(piece_block(p), PB), :, 0:HE],
                               mix_ps[:, :].rearrange("p (n h e) -> p n h e", n=PB, e=HE), ACT.Copy)\
                    .then_inc(S["suf_done"], 1)
                act.wait_ge(S["z_done"], p + 1)
                if not first:
                    act.wait_ge(S["sig_done"], p)
                act.activation(th[:, :, :], z[:, :, :], ACT.Tanh, scale=0.5).then_inc(S["th_done"], 1)

            prepare(0, True)
            with act.Fori(1, PIECES) as p:
                prepare(p)

            def diag_copy(n, t, first=False):
                k = sum(v[0] for v in SU[:n])
                act.wait_ge(S["s_full"], NSU * t + n + 1)
                if k >= 4 or not first:
                    act.wait_ge(S["diag_reduced"], 4 * t + k // 2 - 1)
                act.activation(diag[:, k // 2 % 2, k % 2, :, :],
                               s_ps[:, n % 2, :].rearrange("p (h k) -> p h k", h=G), ACT.Copy)\
                    .then_inc(S["diag_copied"], 1)

            def weights0(half, par, t):
                act.wait_ge(S["top_ready"], 2 * t + (1 if half else 2))
                act.activation(e0[:, par, half, :, :], top[:, half, :, :], ACT.Exp, scale=-SCALE).then_inc(S["e0_ready"], 1)

            def rows_copy(half, t):
                act.wait_ge(S["rows_full"], 2 * t + (1 if half else 2))
                act.activation(top_t[:, half, :], mixb_ps[0:NP3 * G, 0:PT], ACT.Copy)\
                    .then_inc(S["rows_copied"], 1)

            def step(u, par, first=False, last=False):
                t = 2 * u + par
                for what, *of in ORDER:
                    if what == "AU":
                        n, = of
                        half, kb, heads, q0, nq = AU[n]
                        act.wait_ge(S["st_full"], NAU * t + n + 1)
                        if not (first and n < RING):
                            m, back = (n - RING, 0) if n >= RING else (n - RING + NAU, 1)
                            pv = PV.index((AU[m][0], AU[m][1]))
                            act.wait_ge(S["pv_done"], NPV * (t - back) + pv + 1)
                        w = len(heads) // 2 * nq
                        act.activation(probs[:, n % RING, :].rearrange("p (a c) -> p a c", a=2)[:, :, 0:w],
                                       st_ps[:, n % 2, :, 0:w], ACT.Exp, scale=SCALE).then_inc(S["exp_done"], 1)
                    elif what == "SU" and not last and SU[of[0]][0]:
                        diag_copy(of[0], t + 1)
                    elif what == "MAX" and not (of[1] and last):
                        weights0(of[0], (par + of[1]) % 2, t + of[1])
                    elif what == "ROWS" and not (of[1] and last):
                        rows_copy(of[0], t + of[1])
                    elif what == "OUT":
                        half, = of
                        act.wait_ge(S["pv_done"], NPV * t + (8 if half else NPV))
                        if not first:
                            act.wait_ge(S["sums_full"], 2 * t - (1 if half else 0))
                        act.activation(sums_t[:, half, :], pv_ps[:, :], ACT.Copy).then_inc(S["sums_copied"], 1)

            for n in range(NSU):
                if SU[n][0]:
                    diag_copy(n, 0, True)
                if n + 1 == HALF1:
                    weights0(1, 0, 0)
            rows_copy(1, 0)
            step(0, 0, True)
            step(0, 1)
            with act.Fori(1, STEPS // 2 - 1) as u:
                step(u, 0)
                step(u, 1)
            step(STEPS // 2 - 1, 0)
            step(STEPS // 2 - 1, 1, last=True)

            def finish(p):
                act.wait_ge(S["ot_full"], p + 1)
                act.activation(o_t[:, :], mix_ps[:, :], ACT.Copy).then_inc(S["ot_copied"], 1)

            finish(0)
            with act.Fori(1, PIECES) as p:
                finish(p)

        @block.tensor
        def _(pe):
            pe.wait_ge(S["pool_const"], 4)
            pe.wait_ge(S["wf_scaled"], 1)
            pe.transpose(mix_ps[:, 0:P], wf_dq[:, :], ident[:, :]).then_inc(S["wf_full"], 1)
            pe.wait_ge(S["wbd_ready"], 6)
            pe.wait_ge(S["wf_ready"], 1)

            def prepare(p, first=False):
                pe.wait_ge(S["xn_ready"], PB * p + PB)
                if not first:
                    pe.wait_ge(S["z_done"], p)
                for i in range(PB):
                    mm = pe.transpose(mix_ps[:, P * i:P * (i + 1)], xn[:, i, :], ident[:, :])
                mm.then_inc(S["xt_full"], 1)
                pe.wait_ge(S["xt_copied"], p + 1)
                for side in range(2):
                    if side:
                        pe.wait_ge(S["qk_hi"], 2 * p + 1)
                        pe.wait_ge(S["qk_float"], 2 * p + 1)
                    pe.matmul(mix_ps[:, :], wbd[:, side, :], xn_t[:, :], start=True, stop=True)\
                        .then_inc(S["qk_full"], 1)
                pe.wait_ge(S["qk_hi"], 2 * p + 2)
                pe.wait_ge(S["qk_float"], 2 * p + 2)
                for i in range(PB):
                    mm = pe.matmul(mix_ps[:, P * i:P * (i + 1)], xn_t[:, P * i:P * (i + 1)], wbd[:, 2, :],
                                   start=True, stop=True)
                mm.then_inc(S["v_full"], 1)
                pe.wait_ge(S["v_done"], p + 1)
                for i in range(PB):
                    mm = pe.transpose(mix_ps[:, P * i:P * (i + 1)], v_p[:, i, :], ident[:, :])
                mm.then_inc(S["vt_full"], 1)
                pe.wait_ge(S["scanned"], p + 1)
                for i in range(PB):
                    mm = pe.transpose(mix_ps[:, P * i:P * (i + 1)], suf_t[:, P * i:P * (i + 1)], ident[:, :])
                mm.then_inc(S["suf_full"], 1)
                pe.wait_ge(S["suf_done"], p + 1)
                pe.wait_ge(S["xdq_done"], p + 1)
                for i in range(PB):
                    mm = pe.matmul(mix_ps[:, P * i:P * (i + 1)], x_dq[:, P * i:P * (i + 1)], wf_t[:, :],
                                   start=True, stop=True)
                mm.then_inc(S["ffn_full"], 1)

            prepare(0, True)
            with pe.Fori(1, PIECES) as p:
                prepare(p)
            pe.wait_ge(S["z_done"], PIECES)

            def scores(n, par, t, first=False):
                is_diag, i, heads, k0, nk = SU[n]
                if not (first and n < 2):
                    m, back = (n - 2, 0) if n >= 2 else (n - 2 + NSU, 1)
                    before = sum(v[0] == SU[m][0] for v in SU[:m]) + 1
                    if SU[m][0]:
                        pe.wait_ge(S["diag_copied"], NSD * (t - back) + before)
                    else:
                        pe.wait_ge(S["s_reduced"], NSR * (t - back) + before)
                w = nk * P
                for c, h in enumerate(heads):
                    mm = pe.matmul(s_ps[:, n % 2, c * w:(c + 1) * w], q_op[0:MROW, par, h, P * i:P * (i + 1)],
                                   k_op[0:MROW, par, h, P * k0:P * (k0 + nk)], start=True, stop=True)
                mm.then_inc(S["s_full"], 1)

            def rows(half, t, first=False):
                pe.wait_ge(S["low_ready"], 2 * t + (1 if half else 2))
                if not first:
                    pe.wait_ge(S["num_done"], 2 * t - (1 if half else 0))
                    pe.wait_ge(S["rows_copied"], 2 * t + (0 if half else 1))
                for i in range(4):
                    mm = pe.transpose(mixb_ps[0:NP3 * G, P * i:P * (i + 1)], top_p[:, half, i, :, :],
                                      identb[:, :])
                mm.then_inc(S["rows_full"], 1)

            def step(u, par, first=False, last=False):
                t = 2 * u + par
                for what, *of in ORDER:
                    if what == "AU":
                        n, = of
                        half, kb, heads, q0, nq = AU[n]
                        if not (first and n < 2):
                            pe.wait_ge(S["exp_done"], NAU * t + n - 1)
                        if n == 0 or (n and AU[n - 1][0] != half):
                            pe.wait_ge(S["rows_loaded"], 32 * t + (16 if half else 32))
                        per = len(heads) // 2
                        for c, h in enumerate(heads):
                            mm = pe.matmul(st_ps[:, n % 2, c // per, c % per * nq:(c % per + 1) * nq],
                                           k_op[:, par, h, P * kb:P * (kb + 1)],
                                           q_op[:, par, h, q0:q0 + nq], start=True, stop=True)
                        mm.then_inc(S["st_full"], 1)
                    elif what == "PV":
                        half, kb = PV[of[0]]
                        mine = [n for n, v in enumerate(AU) if (v[0], v[1]) == (half, kb)]
                        pe.wait_ge(S["exp_done"], NAU * t + mine[-1] + 1)
                        if mine[-1] in MASKED:
                            pe.wait_ge(S["masked"], NMASK * t + MASKED.index(mine[-1]) + 1)
                        if of[0] == 0:
                            pe.wait_ge(S["v_op_ready"], t + 1)
                        if kb == 0 and not (first and half):
                            pe.wait_ge(S["sums_copied"], 2 * t + (0 if half else 1))
                        for n in mine:
                            _, _, heads, q0, nq = AU[n]
                            per = len(heads) // 2
                            tile = probs[:, n % RING, :].rearrange("p (a c) -> p a c", a=2)
                            for c, h in enumerate(heads):
                                mm = pe.matmul(pv_ps[32 * h:32 * (h + 1), q0 - half * PT:q0 - half * PT + nq],
                                               v_op[:, par, kb, h, :],
                                               tile[:, c // per, c % per * nq:(c % per + 1) * nq],
                                               start=(kb == 0), stop=(kb == 4 * half + 3),
                                               skip_group_check=True)
                        mm.then_inc(S["pv_done"], 1)
                    elif what == "OUT":
                        half, = of
                        pe.wait_ge(S["sums_copied"], 2 * t + (1 if half else 2))
                        pe.wait_ge(S["rows_copied"], 2 * t + (2 if half or last else 3))
                        if not (first and half):
                            pe.wait_ge(S["num_done"], 2 * t + (0 if half else 1))
                        for i in range(4):
                            mm = pe.transpose(mix_ps[:, P * i:P * (i + 1)], sums_t[:, half, P * i:P * (i + 1)],
                                              ident[:, :])
                        mm.then_inc(S["sums_full"], 1)
                    elif what == "SU" and not last:
                        if of[0] == 0:
                            pe.wait_ge(S["q_loaded"], 384 * (t + 2))
                        scores(of[0], 1 - par, t + 1)
                    elif what == "ROWS" and not (of[1] and last):
                        rows(of[0], t + of[1])

            pe.wait_ge(S["q_loaded"], 384)
            for n in range(NSU):
                scores(n, 0, 0, True)
            rows(1, 0, True)
            step(0, 0, True)
            step(0, 1)
            with pe.Fori(1, STEPS // 2 - 1) as u:
                step(u, 0)
                step(u, 1)
            step(STEPS // 2 - 1, 0)
            step(STEPS // 2 - 1, 1, last=True)
            pe.wait_ge(S["num_done"], 2 * STEPS)

            def finish(p, first=False):
                pe.wait_ge(S["o_done"], p + 1)
                if not first:
                    pe.wait_ge(S["y1_done"], p)
                for i in range(PB):
                    mm = pe.transpose(mix_ps[:, P * i:P * (i + 1)], o_p[:, i, :], ident[:, :])
                mm.then_inc(S["ot_full"], 1)
                pe.wait_ge(S["ot_copied"], p + 1)
                for i in range(PB):
                    mm = pe.matmul(mix_ps[:, P * i:P * (i + 1)], o_t[:, P * i:P * (i + 1)], wr_sb[:, :],
                                   start=True, stop=True)
                mm.then_inc(S["y_full"], 1)

            finish(0, True)
            with pe.Fori(1, PIECES) as p:
                finish(p)

        @block.vector
        def _(dve):
            dve.memset(v_all[:, :, :, HE:VC], 1.0).then_inc(S["setup_dve"], 1)
            dve.memset(carry[:, :], 0.0).then_inc(S["setup_dve"], 1)
            dve.memset(tops[:, :, :, :, :], 0.0).then_inc(S["setup_dve"], 1)
            dve.memset(v_op[:, :, :, :, :], 0.0).then_inc(S["setup_dve"], 1)
            for n in range(NBLK):
                if n % CB == 0:
                    dve.wait_ge(S[f"x_loaded{n // CB}"], 16)
                dve.bn_stats(stats[:, n, :], x_all[:, n, :]).then_inc(S["stats_done"], 1)
            dve.wait_ge(S["stats_done"], NBLK)
            dve.tensor_tensor(mean2[:, :], stats[:, :, 1], stats[:, :, 4], ALU.add).then_inc(S["mean_done"], 1)
            dve.tensor_tensor(dev[:, :], stats[:, :, 1], stats[:, :, 4], ALU.subtract).then_inc(S["mean_done"], 1)
            dve.tensor_tensor(m2[:, :], stats[:, :, 2], stats[:, :, 5], ALU.add).then_inc(S["mean_done"], 1)
            dve.wait_ge(S["mean_done"], 3)
            dve.tensor_scalar(mean[:, :], mean2[:, :], 0.5, None, ALU.mult).then_inc(S["mean_done"], 1)
            dve.tensor_tensor(dev2[:, :], dev[:, :], dev[:, :], ALU.mult).then_inc(S["mean_done"], 1)
            dve.wait_ge(S["mean_done"], 5)
            dve.scalar_tensor_tensor(out=var[:, :], in0=dev2[:, :], scalar=D / 4.0, in1=m2[:, :], op0=ALU.mult,
                                     op1=ALU.add).then_inc(S["mean_done"], 1)
            dve.wait_ge(S["mean_done"], 6)
            dve.tensor_scalar(vareps[:, :], var[:, :], 1.0 / D, EPS, ALU.mult, ALU.add).then_inc(S["norm_ready"], 1)
            dve.wait_ge(S["sqrt_done"], 1)
            dve.reciprocal(rstd[:, :], std[:, :]).then_inc(S["mean_done"], 1)
            dve.wait_ge(S["weights_loaded"], 144)
            dve.tensor_scalar(wf_dq[:, :], wf_raw[:, :], wsc[:, 0:1], None, ALU.mult).then_inc(S["wf_scaled"], 1)
            dve.reciprocal(risc[:, :], isc[:, :]).then_inc(S["mean_done"], 1)
            dve.wait_ge(S["pool_const"], 5)
            dve.tensor_copy(count[:, :], count_i[:, :]).then_inc(S["mean_done"], 1)
            dve.wait_ge(S["mean_done"], 9)
            for b in range(B):
                dve.tensor_copy(num[:, CB * b:CB * (b + 1), :, HE],
                                count[:, :].rearrange("p (n a) -> p n a", a=1).to_broadcast([P, CB, H]))\
                    .then_inc(S["setup_dve"], 1)

            def prepare(p, first=False):
                blk = piece_block(p)
                if not first:
                    dve.wait_ge(S["xt_full"], p)
                for i in range(PB):
                    dve.tensor_scalar(xn[:, i, :], x_all[:, bass.ds(blk + i, 1), :],
                                      mean[:, bass.ds(blk + i, 1)], rstd[:, bass.ds(blk + i, 1)],
                                      ALU.subtract, ALU.mult).then_inc(S["xn_ready"], 1)
                for side in range(2):
                    dve.wait_ge(S["qk_full"], 2 * p + side + 1)
                    if not first:
                        dve.wait_ge(S["qk_res"], 2 * p)
                    dve.wait_ge(S["qk_hi"], 2 * p + side + 1)
                    dve.tensor_scalar(qk_f[:, side, :], mix_ps[:, :], bqk[:, side:side + 1], None, ALU.add)\
                        .then_inc(S["qk_float"], 1)
                dve.wait_ge(S["v_full"], p + 1)
                if not first:
                    dve.wait_ge(S["v_copied"], p)
                dve.tensor_tensor(v_p[:, :, :], mix_ps[:, :].rearrange("p (n d) -> p n d", n=PB),
                                  bv[:, :].rearrange("p (a d) -> p a d", a=1).to_broadcast([P, PB, D]), ALU.add)\
                    .then_inc(S["v_done"], 1)
                dve.wait_ge(S["vt_full"], p + 1)
                if not first:
                    dve.wait_ge(S["suf_full"], p)
                    dve.wait_ge(S["carry_done"], p)
                else:
                    dve.wait_ge(S["setup_dve"], 4 + B)
                dve.tensor_tensor_scan(suf_t[:, ::-1], mix_ps[:, ::-1], xn_t[:, :],
                                       carry[:, bass.ds(piece_carry(p), 1)], ALU.add, ALU.bypass)\
                    .then_inc(S["scanned"], 1)
                dve.wait_ge(S["scanned"], p + 1)
                dve.tensor_copy(carry[:, bass.ds(piece_carry(p) + 1, 1)],
                                suf_t[:, 0:1]).then_inc(S["carry_done"], 1)
                if not first:
                    dve.wait_ge(S["fine_done"], p)
                    dve.wait_ge(S["half_done"], p)
                dve.tensor_scalar(xs[:, :], xn_t[:, :], risc[:, 0:1], None, ALU.mult).then_inc(S["xs_done"], 1)
                dve.wait_ge(S["xs_done"], p + 1)
                dve.tensor_scalar(xs_half[:, :], xs[:, :], 0.5, None, ALU.mult).then_inc(S["half_done"], 1)
                if not first:
                    wait_apart(dve, S["far_done"], p)
                dve.tensor_scalar(x_fine[:, :], xs[:, :], FINE, -FINE, ALU.min, ALU.max, saturate=False)\
                    .then_inc(S["fine_done"], 1)
                wait_apart(dve, S["half_done"], p + 1)
                dve.tensor_scalar(x_pos[:, :], xs_half[:, :], FINE / 2, FP8_MAX / 2, ALU.max, ALU.min,
                                  saturate=False)\
                    .then_inc(S["pos_done"], 1)
                dve.tensor_scalar(x_neg[:, :], xs_half[:, :], -FINE / 2, -FP8_MAX / 2, ALU.min, ALU.max,
                                  saturate=False)\
                    .then_inc(S["neg_done"], 1)
                wait_apart(dve, S["neg_done"], p + 1)
                wait_apart(dve, S["pos_done"], p + 1)
                dve.tensor_tensor(x_far[:, :], x_pos[:, :], x_neg[:, :], ALU.add).then_inc(S["far_done"], 1)
                wait_apart(dve, S["far_done"], p + 1)
                wait_apart(dve, S["fine_done"], p + 1)
                dve.scalar_tensor_tensor(out=x_q[:, :], in0=x_far[:, :], scalar=2.0, in1=x_fine[:, :],
                                         op0=ALU.mult, op1=ALU.add).then_inc(S["xq_done"], 1)
                dve.wait_ge(S["xq_done"], p + 1)
                if not first:
                    dve.wait_ge(S["ffn_full"], p)
                dve.tensor_scalar(x_dq[:, :], x_q[:, :], isc[:, 0:1], None, ALU.mult).then_inc(S["xdq_done"], 1)
                dve.wait_ge(S["ffn_full"], p + 1)
                if not first:
                    dve.wait_ge(S["gate_done"], p)
                dve.tensor_tensor(z[:, :, :], mix_ps[:, :].rearrange("p (n d) -> p n d", n=PB),
                                  bf_sb[:, :].rearrange("p (a d) -> p a d", a=1).to_broadcast([P, PB, D]), ALU.add)\
                    .then_inc(S["z_done"], 1)
                dve.wait_ge(S["th_done"], p + 1)
                dve.tensor_scalar(sig[:, :, :], th[:, :, :], 0.5, 0.5, ALU.mult, ALU.add).then_inc(S["sig_done"], 1)

            dve.wait_ge(S["mean_done"], 9)
            prepare(0, True)
            with dve.Fori(1, PIECES) as p:
                prepare(p)

            def reduce(n, t, first=False):
                is_diag, i, heads, k0, nk = SU[n]
                half = i // 4
                if is_diag:
                    return
                r = n - sum(v[0] for v in SU[:n])
                dve.wait_ge(S["s_full"], NSU * t + n + 1)
                slot = 0 if k0 == 0 else 1
                dve.tensor_reduce(tops[:, half, i % 4, heads[0]:heads[-1] + 1, slot],
                                  s_ps[:, n % 2, 0:len(heads) * nk * P].rearrange("p (h k) -> p h k", h=len(heads)),
                                  AX.X, ALU.max).then_inc(S["s_reduced"], 1)

            def reduce_diag(k, t):
                half, i = (1, 0) if k < 2 else (0, 0)
                i = 2 * (k % 2)
                dve.wait_ge(S["diag_masked"], 4 * t + k + 1)
                dve.tensor_reduce(tops[:, half, i:i + 2, :, 2],
                                  diag[:, k % 2, :, :, :], AX.X, ALU.max).then_inc(S["diag_reduced"], 1)

            def maxima(half, t, first=False):
                n = 2 * t + (1 if half else 2)
                dve.wait_ge(S["s_reduced"], NSR * t + (sum(not v[0] for v in SU[:HALF1]) if half else NSR))
                dve.wait_ge(S["diag_reduced"], 4 * t + (2 if half else 4))
                if not first:
                    dve.wait_ge(S["e0_ready"], n - 2)
                    dve.wait_ge(S["rows_full"], n - 2)
                dve.tensor_reduce(top[:, half, :, :], tops[:, half, :, :, :], AX.X, ALU.max)\
                    .then_inc(S["top_ready"], 1)
                dve.wait_ge(S["top_ready"], n)
                dve.tensor_scalar(top_p[:, half, :, 0, :], top[:, half, :, :], -1.0, None, ALU.mult)\
                    .then_inc(S["hi_ready"], 1)
                dve.wait_ge(S["hi_ready"], n)
                dve.scalar_tensor_tensor(out=top_r[:, half, :, :], in0=top[:, half, :, :], scalar=-1.0,
                                         in1=top_p[:, half, :, 0, :], op0=ALU.mult, op1=ALU.subtract)\
                    .then_inc(S["res_ready"], 1)
                dve.wait_ge(S["res_ready"], n)
                dve.tensor_copy(top_p[:, half, :, 1, :], top_r[:, half, :, :]).then_inc(S["mid_ready"], 1)
                dve.wait_ge(S["mid_ready"], n)
                dve.tensor_tensor(top_p[:, half, :, 2, :], top_r[:, half, :, :], top_p[:, half, :, 1, :], ALU.subtract)\
                    .then_inc(S["low_ready"], 1)

            def step(u, par, first=False, last=False):
                t = 2 * u + par
                b, h = step_batch(u), step_head(u, par)
                for what, *of in ORDER:
                    if what == "SU" and not last:
                        n, = of
                        reduce(n, t + 1)
                        if n in DIAG_AFTER:
                            reduce_diag(DIAG_AFTER[n], t + 1)
                    elif what == "MAX" and not (of[1] and last):
                        maxima(of[0], t + of[1], first and not of[1] or first)
                    elif what == "OUT":
                        half, = of
                        n = 2 * t + (1 if half else 2)
                        mine = num[:, bass.ds(8 * b + 4 * half, 4), bass.ds(h, G), :]
                        dve.wait_ge(S["e0_ready"], n)
                        if not first:
                            dve.wait_ge(S["num_done"], n - 2)
                        dve.tensor_tensor(scaled[:, half, :, :, :], mine,
                                          e0[:, par, half, :, :].rearrange("p i (h a) -> p i h a", a=1)
                                          .to_broadcast([P, 4, G, VC]), ALU.mult).then_inc(S["scaled_done"], 1)
                        dve.wait_ge(S["sums_full"], n)
                        dve.wait_ge(S["scaled_done"], n)
                        dve.tensor_tensor(mine, scaled[:, half, :, :, :],
                                          mix_ps[:, :].rearrange("p (i h c) -> p i h c", i=4, h=G)[:, :, :, 0:VC],
                                          ALU.add).then_inc(S["num_done"], 1)

            for n in range(NSU):
                reduce(n, 0, True)
                if n in DIAG_AFTER:
                    reduce_diag(DIAG_AFTER[n], 0)
                if n + 1 == HALF1:
                    maxima(1, 0, True)
            step(0, 0, True)
            step(0, 1)
            with dve.Fori(1, STEPS // 2 - 1) as u:
                step(u, 0)
                step(u, 1)
            step(STEPS // 2 - 1, 0)
            step(STEPS // 2 - 1, 1, last=True)

            def finish(p, first=False):
                blk = piece_block(p)
                if first:
                    dve.wait_ge(S["num_done"], 2 * STEPS)
                else:
                    dve.wait_ge(S["o_done"], p)
                dve.reciprocal(rden[:, :, :], num[:, bass.ds(blk, PB), :, HE]).then_inc(S["den_inverted"], 1)
                dve.wait_ge(S["y_full"], p + 1)
                if not first:
                    dve.wait_ge(S["y2_done"], p)
                dve.tensor_tensor(y1[:, :, :], mix_ps[:, :].rearrange("p (n d) -> p n d", n=PB),
                                  br_sb[:, :].rearrange("p (a d) -> p a d", a=1).to_broadcast([P, PB, D]), ALU.add)\
                    .then_inc(S["y1_done"], 1)
                dve.wait_ge(S["y1_done"], p + 1)
                dve.tensor_tensor(y2[:, :, :], y1[:, :, :], gate[:, bass.ds(blk, PB), :], ALU.mult)\
                    .then_inc(S["y2_done"], 1)
                dve.wait_ge(S["y2_done"], p + 1)
                if not first:
                    dve.wait_ge(S["stored"], 16 * p)
                dve.tensor_tensor(y3[:, :, :], y2[:, :, :], x_all[:, bass.ds(blk, PB), :], ALU.add)\
                    .then_inc(S["y3_done"], 1)

            finish(0, True)
            with dve.Fori(1, PIECES) as p:
                finish(p)

        @block.gpsimd
        def _(pool):
            pool.memset(ident[:, :], 0.0).then_inc(S["pool_const"], 1)
            pool.wait_ge(S["pool_const"], 1)
            pool.affine_select(out=ident[:, :], in_=ident[:, :], compare_op=ALU.not_equal, fill=1.0, base=0,
                               pattern=[[-1, P]], channel_multiplier=1).then_inc(S["pool_const"], 1)
            pool.wait_ge(S["pool_const"], 2)
            pool.tensor_copy(identb[:, :], ident[:, :]).then_inc(S["pool_const"], 1)
            pool.wait_ge(S["pool_const"], 3)
            pool.memset(q_op[64:128, :, :, :].bitcast(F32), 0.0).then_inc(S["rows_set"], 1)
            pool.wait_ge(S["rows_set"], 1)
            pool.memset(k_op[64:128, :, :, :].bitcast(F32), 0.0).then_inc(S["rows_set"], 1)
            pool.wait_ge(S["rows_set"], 2)
            pool.memset(k_op[MROW:MROW + NP3, :, :, :], 1.0).then_inc(S["pool_const"], 1)
            pool.wait_ge(S["pool_const"], 4)
            pool.iota(count_i[:, :], pattern=[[-P, CB]], base=C, channel_multiplier=-1)\
                .then_inc(S["pool_const"], 1)
            pool.wait_ge(S["wrep_loaded"], 16)
            for m in range(3):
                src = wrep[:, HE * m:HE * (m + 1)].rearrange("p (a f) -> p a f", a=1).to_broadcast([P, H, HE])
                pool.affine_select(out=wbd_half[:, m, :].rearrange("p (h f) -> p h f", h=H), in_=src,
                                   compare_op=ALU.is_ge, fill=0.0, base=0, pattern=[[-HE, H], [0, HE]],
                                   channel_multiplier=1).then_inc(S["wbd_ready"], 1)
            pool.wait_ge(S["wbd_ready"], 3)
            for m in range(3):
                last = pool.affine_select(out=wbd[:, m, :].rearrange("p (h f) -> p h f", h=H),
                                          in_=wbd_half[:, m, :].rearrange("p (h f) -> p h f", h=H),
                                          compare_op=ALU.is_ge, fill=0.0, base=HE - 1,
                                          pattern=[[HE, H], [0, HE]], channel_multiplier=-1)
                last.then_inc(S["wbd_ready"], 1)
            pool.wait_ge(S["weights_loaded"], 144)

            def prepare(p, first=False):
                for side in range(2):
                    n = 2 * p + side + 1
                    pool.wait_ge(S["qk_float"], n)
                    pool.wait_ge(S["qk_hi"], n)
                    pool.tensor_tensor(qk_p[:, side, 1, :], qk_f[:, side, :], qk_p[:, side, 0, :], ALU.subtract)\
                        .then_inc(S["qk_mid"], 1)
                    if not first:
                        pool.wait_ge(S["qk_low"], n - 2)
                    pool.tensor_tensor(qk_r[:, side, :], qk_f[:, side, :], qk_p[:, side, 0, :], ALU.subtract)\
                        .then_inc(S["qk_res"], 1)
                    pool.wait_ge(S["qk_mid"], n)
                    pool.wait_ge(S["qk_res"], n)
                    pool.tensor_tensor(qk_p[:, side, 2, :], qk_r[:, side, :], qk_p[:, side, 1, :], ALU.subtract)\
                        .then_inc(S["qk_low"], 1)
                pool.wait_ge(S["sig_done"], p + 1)
                pool.tensor_tensor(gate[:, bass.ds(piece_block(p), PB), :], z[:, :, :], sig[:, :, :], ALU.mult)\
                    .then_inc(S["gate_done"], 1)

            prepare(0, True)
            with pool.Fori(1, PIECES) as p:
                prepare(p)

            def mask_diag(k, t):
                wait_apart(pool, S["diag_copied"], NSD * t + 2 * k + 2)
                tile = diag[:, k % 2, :, :, :].rearrange("p i h k -> p (i h) k")
                pool.affine_select(out=tile, in_=tile, compare_op=ALU.is_gt, fill=0.0, base=0,
                                   pattern=[[0, 2 * G], [-1, P]], channel_multiplier=1)\
                    .then_inc(S["diag_masked"], 1)

            def load_v(u, par, first=False):
                t = 2 * u + par
                if not first:
                    pool.wait_ge(S["pv_done"], NPV * (t - 1))
                pool.tensor_copy(v_op[:, par, :, :, 0:VC],
                                 v_all[:, bass.ds(CB * step_batch(u), CB), bass.ds(step_head(u, par), G), :])\
                    .then_inc(S["v_op_ready"], 1)

            def step(u, par, first=False, last=False, load=True):
                t = 2 * u + par
                for what, *of in ORDER:
                    if what == "AU" and of[0] in MASKED:
                        n, = of
                        half, kb, heads, q0, nq = AU[n]
                        per = len(heads) // 2
                        wait_apart(pool, S["exp_done"], NAU * t + n + 1)
                        for a in range(2):
                            tile = probs[:, n % RING, a * PT:a * PT + per * nq]\
                                .rearrange("p (c q) -> p c q", c=per)[:, :, 0:P]
                            last_op = pool.affine_select(out=tile, in_=tile, compare_op=ALU.is_gt, fill=0.0,
                                                         base=0, pattern=[[0, per], [1, P]],
                                                         channel_multiplier=-1)
                        last_op.then_inc(S["masked"], 1)
                    elif what == "SU" and not last and of[0] in MASK_AFTER:
                        mask_diag(MASK_AFTER[of[0]], t + 1)
                if load:
                    load_v(u + 1, par)

            pool.wait_ge(S["v_copied"], PIECES)
            pool.wait_ge(S["setup_dve"], 4)
            load_v(0, 0, True)
            load_v(0, 1, True)
            for n in range(NSU):
                if n in MASK_AFTER:
                    mask_diag(MASK_AFTER[n], 0)
            step(0, 0, True)
            step(0, 1)
            with pool.Fori(1, STEPS // 2 - 1) as u:
                step(u, 0)
                step(u, 1)
            step(STEPS // 2 - 1, 0, load=False)
            step(STEPS // 2 - 1, 1, last=True, load=False)

            def finish(p, first=False):
                mine = num[:, bass.ds(piece_block(p), PB), :, :]
                if not first:
                    pool.wait_ge(S["ot_full"], p)
                pool.wait_ge(S["den_inverted"], p + 1)
                pool.tensor_tensor(o_p[:, :, :].rearrange("p n (h e) -> p n h e", e=HE), mine[:, :, :, 0:HE],
                                   rden[:, :, :].rearrange("p n (h a) -> p n h a", a=1)
                                   .to_broadcast([P, PB, H, HE]), ALU.mult)\
                    .then_inc(S["o_done"], 1)

            finish(0, True)
            with pool.Fori(1, PIECES) as p:
                finish(p)


MASK_AFTER = {n: k for k, n in enumerate([n for n, u in enumerate(SU) if u[0]][1::2])}
DIAG_AFTER = {min(n + 4, (HALF1 if n < HALF1 else NSU) - 1): k for n, k in MASK_AFTER.items()}


_INS = ["L0_attn_x", "L0_attn_Wqkv", "L0_attn_bqkv", "L0_attn_Wr", "L0_attn_br", "L0_ffn_weight_fp8",
        "L0_ffn_bias", "L0_ffn_input_scale", "L0_ffn_weight_scale"]


def kernel(**inputs):
    import concourse.bacc as bacc
    from concourse.bass_utils import run_bass_kernel_spmd

    nc = bacc.Bacc("TRN2", target_bir_lowering=False, num_devices=1)
    arrays, args = {}, []
    for name in _INS:
        a = np.ascontiguousarray(inputs[name])
        arrays[name] = a
        args.append(nc.dram_tensor(name, a.shape, mybir.dt.from_np(a.dtype), kind="ExternalInput").ap())
    args.append(nc.dram_tensor("out", (B, C, D), F32, kind="ExternalOutput").ap())
    program(nc, *args)
    r = run_bass_kernel_spmd(nc, [arrays], core_ids=[0])
    return r.results[0]["out"]
```

```python
from contextlib import ExitStack

import numpy as np

import concourse.bass as bass
from concourse import mybir

F32 = mybir.dt.float32
BF16 = mybir.dt.bfloat16
FP8 = mybir.dt.float8e4
I32 = mybir.dt.int32
ALU = mybir.AluOpType
ACT = mybir.ActivationFunctionType
AX = mybir.AxisListType

P = 128
B, C, D, H = 4, 1024, 128, 16
HE = D // H
TOK = B * C
NBLK = TOK // P
CB = C // P
G = 4
NG = H // G
STEPS = B * NG
PT = 512
PB = PT // P
PIECES = TOK // PT
NP3 = 3
ROWS = NP3 * NP3 * HE
MROW = 96
VC = HE + 1
SCALE = float(1.0 / np.sqrt(np.float32(HE)))
EPS = 1e-5
FP8_MAX = 448.0
FINE = 16.0



def score_units():
    units = []
    for half in (1, 0):
        blocks = range(half * 4, half * 4 + 4)
        units += [(True, i, (0, 1, 2, 3), i, 1) for i in blocks]
        for i in reversed(blocks):
            rest, first = i % 4, i - i % 4
            if rest == 3:
                units += [(False, i, (h,), first, 3) for h in range(G)]
            elif rest:
                per = 4 // rest
                units += [(False, i, tuple(range(h, h + per)), first, rest) for h in range(0, G, per)]
        for i in reversed(blocks):
            if i >= 4:
                units += [(False, i, (h,), 0, 4) for h in range(G)]
    return units


def attend_units():
    units = []
    for half in (1, 0):
        for kb in range(4 * half + 4):
            q0 = max(half * PT, kb * P)
            n = (half + 1) * PT - q0
            for heads in (((0, 1), (2, 3)) if n > PT // 2 else ((0, 1, 2, 3),)):
                units.append((half, kb, heads, q0, n))
    return units


SU = score_units()
AU = attend_units()
NSU, NAU = len(SU), len(AU)
NSD = sum(u[0] for u in SU)
NSR = NSU - NSD
HALF1 = max(n for n, u in enumerate(SU) if u[1] >= 4) + 1
HALF1_R = sum(not u[0] for u in SU[:HALF1])
LOWER = min(n for n, u in enumerate(SU) if u[3] < 4)
AHALF1 = sum(u[0] for u in AU)
PV = [(half, kb) for half in (1, 0) for kb in range(4 * half + 4)]
NPV = len(PV)
PV_UNITS = [[n for n, u in enumerate(AU) if (u[0], u[1]) == pv] for pv in PV]
PV_OF = [PV.index((u[0], u[1])) for u in AU]
MASKED = [n for n, (half, kb, _, q0, _) in enumerate(AU) if q0 == kb * P]
NMASK = len(MASKED)
RING = 5
LAG = 2
MASK_AFTER = {n: k for k, n in enumerate([n for n, u in enumerate(SU) if u[0]][1::2])}
DIAG_AFTER = {min(n + 4, (HALF1 if n < HALF1 else NSU) - 1): k for n, k in MASK_AFTER.items()}

PREPARE = (
    {0: ["norm"], 1: ["fill xt"], 2: ["read xt"], 4: ["fill q"], 5: ["read q"], 7: ["fill k"], 8: ["read k"],
     12: ["quantise"], 13: ["split"]},
    {0: ["fill v"], 1: ["read v"], 5: ["fill vt"], 6: ["read vt"], 8: ["fill suf"], 9: ["read suf"],
     11: ["fill ffn"], 12: ["read ffn"]},
)
FINISH = (
    {9: ["divide"], 11: ["fill ot"], 12: ["read ot"], 15: ["fill y"], 17: ["read y"]},
    {},
)


def step_order(parity):
    order, s, m = [], 0, 0
    for n in range(NAU + LAG + 1):
        if n < NAU:
            order.append(("AU", n))
        if n == 0:
            order.append(("MAX", 0, 0))
        if n == 2:
            order.append(("FILL", "rows", 0, 0))
        if n == 3:
            order.append(("READ", "rows", 0, 0))
        upto = -(-HALF1 * min(n + 1, AHALF1) // AHALF1) if n < AHALF1 else min(NSU, HALF1 + 2 * (n - AHALF1 + 1))
        while s < upto:
            order.append(("SU", s))
            s += 1
            if s == HALF1:
                order.append(("MAX", 1, 1))
        while m < NPV and PV_UNITS[m][-1] + LAG <= n:
            order.append(("PV", m))
            m += 1
            if m == NPV or PV[m][0] != PV[m - 1][0]:
                order.append(("SUMS", PV[m - 1][0]))
        order += [("PREPARE", stage) for stage in PREPARE[parity].get(n, ())]
        order += [("FINISH", stage) for stage in FINISH[parity].get(n, ())]
        if n == AHALF1:
            order.append(("LOAD", 1))
        if n == AHALF1 + LAG + 1:
            order += [("FILL", "out", 1), ("READ", "out", 1)]
        if n == 18:
            order += [("FILL", "rows", 1, 1), ("LOADV",)]
        if n == 19:
            order += [("READ", "rows", 1, 1), ("LOAD", 0)]
    order += [("FILL", "out", 0), ("READ", "out", 0)]
    assert s == NSU and m == NPV
    return order


ORDER = [step_order(0), step_order(1)]
PREPARE_ALL = [stage for part in PREPARE for n in sorted(part) for stage in part[n]]
FINISH_ALL = [stage for part in FINISH for n in sorted(part) for stage in part[n]]
PAIRS = STEPS // 2
AHEAD = PIECES // B


def program(nc, x, wqkv, bqkv, wr, br, wffn, bffn, iscale, wscale, out):
    ctx = ExitStack()
    with ctx:
        def sb(name, shape, dt=F32):
            return ctx.enter_context(nc.sbuf_tensor(name, shape, dt))

        def ps(name, shape, dt=F32):
            return ctx.enter_context(nc.psum_tensor(name, shape, dt))

        sems = {}

        def sem(name):
            sems[name] = ctx.enter_context(nc.semaphore(name))
            return sems[name]

        split_dram = nc.dram_tensor("split_dram", (2, H, HE, NP3, NP3, TOK), BF16, kind="Internal").ap()
        x_all = sb("x_all", [P, NBLK, D])
        gate = sb("gate", [P, NBLK, D])
        v_all = sb("v_all", [P, NBLK, H, VC])
        num = sb("num", [P, NBLK, H, VC])
        q_op = sb("q_op", [P, 2, G, C], BF16)
        k_op = sb("k_op", [P, 2, G, C], BF16)
        v_op = sb("v_op", [P, 2, CB, G, 32])
        probs = sb("probs", [P, RING, 2 * PT])
        diag = sb("diag", [P, 2, 2, G, P])
        ident = sb("ident", [P, P])
        identb = sb("identb", [P, P], BF16)
        wrep = sb("wrep", [P, 3 * HE])
        wbd = sb("wbd", [P, 3, P])
        wbd_half = sb("wbd_half", [P, 3, P])
        bqk = sb("bqk", [P, 2])
        bv = sb("bv", [P, P])
        wr_sb = sb("wr_sb", [P, D])
        br_sb = sb("br_sb", [P, D])
        wf_raw = sb("wf_raw", [P, D])
        wf_dq = sb("wf_dq", [P, D])
        wf_t = sb("wf_t", [P, D])
        bf_sb = sb("bf_sb", [P, D])
        isc = sb("isc", [P, 1])
        risc = sb("risc", [P, 1])
        wsc = sb("wsc", [P, 1])
        stats = sb("stats", [P, NBLK, 6])
        mean2 = sb("mean2", [P, NBLK])
        mean = sb("mean", [P, NBLK])
        dev = sb("dev", [P, NBLK])
        dev2 = sb("dev2", [P, NBLK])
        m2 = sb("m2", [P, NBLK])
        var = sb("var", [P, NBLK])
        vareps = sb("vareps", [P, NBLK])
        std = sb("std", [P, NBLK])
        rstd = sb("rstd", [P, NBLK])
        count_i = sb("count_i", [P, CB], I32)
        count = sb("count", [P, CB])
        xn = sb("xn", [P, PB, D])
        xn_t = sb("xn_t", [P, PT])
        qk_f = sb("qk_f", [P, 2, PT])
        qk_r = sb("qk_r", [P, 2, PT])
        qk_p = sb("qk_p", [P, 2, NP3, PT], BF16)
        v_p = sb("v_p", [P, PB, D])
        suf_t = sb("suf_t", [P, PT])
        carry = sb("carry", [P, PIECES + B])
        xs = sb("xs", [P, PT])
        xs_half = sb("xs_half", [P, PT])
        x_fine = sb("x_fine", [P, PT], FP8)
        x_pos = sb("x_pos", [P, PT], FP8)
        x_neg = sb("x_neg", [P, PT], FP8)
        x_far = sb("x_far", [P, PT])
        x_q = sb("x_q", [P, PT])
        x_dq = sb("x_dq", [P, PT])
        z = sb("z", [P, PB, D])
        th = sb("th", [P, PB, D])
        sig = sb("sig", [P, PB, D])
        tops = sb("tops", [P, 2, 4, G, 3])
        top = sb("top", [P, 2, 4, G])
        e0 = sb("e0", [P, 2, 2, 4, G])
        top_r = sb("top_r", [P, 2, 4, G])
        top_p = sb("top_p", [P, 2, 4, NP3, G], BF16)
        top_t = sb("top_t", [NP3 * G, 2, PT], BF16)
        sums_t = sb("sums_t", [P, 2, PT])
        scaled = sb("scaled", [P, 2, 4, G, VC])
        rden = sb("rden", [P, PB, H])
        o_p = sb("o_p", [P, PB, D])
        o_t = sb("o_t", [P, PT])
        y1 = sb("y1", [P, PB, D])
        y2 = sb("y2", [P, PB, D])
        y3 = sb("y3", [P, PB, D])

        st_ps = ps("st_ps", [P, 2, 2, PT])
        s_ps = ps("s_ps", [P, 2, PT])
        pv_ps = ps("pv_ps", [P, PT])
        mix_ps = ps("mix_ps", [P, PT])
        mixb_ps = mix_ps[:, :].bitcast(BF16)

        for name in """waited x_loaded0 x_loaded1 x_loaded2 x_loaded3 weights_loaded wrep_loaded
                stats_done mean_done norm_ready sqrt_done setup_dve
                pool_const rows_set wbd_ready wf_scaled wf_full wf_ready
                xn_ready xt_full xt_copied qk_full qk_hi qk_float qk_res qk_mid qk_low split_stored
                v_full v_done v_copied vt_full scanned carry_done suf_full suf_done
                xs_done half_done fine_done pos_done neg_done far_done xq_done xdq_done
                ffn_full z_done th_done sig_done gate_done
                upper_loaded0 upper_loaded1 lower_loaded0 lower_loaded1 s_full diag_copied diag_masked diag_reduced s_reduced
                top_ready e0_ready hi_ready res_ready mid_ready low_ready rows_full rows_copied rows_loaded
                v_op_ready st_full exp_done masked pv_done sums_copied sums_full scaled_done num_done
                den_inverted o_done ot_full ot_copied y_full y1_done y2_done y3_done stored""".split():
            sem(name)
        S = sems

        block = ctx.enter_context(nc.Block())

        def wait_apart(engine, semaphore, value):
            engine.wait_ge(semaphore, value)
            engine.sem_inc(S["waited"], 1)

        def piece_block(p):
            return 8 * (p // 2) + 4 * (1 - p % 2)

        def piece_carry(p):
            return p + p // 2

        def step_batch(u):
            return u // 2

        def step_head(u, par):
            return 8 * (u % 2) + 4 * par

        def run(engine, pair):
            pair(0, prep=True, first=True)
            pair(1, prep=True)
            with engine.Fori(2, PAIRS - 2) as u:
                pair(u, prep=True, fin=True)
            pair(PAIRS - 2, fin=True)
            pair(PAIRS - 1, fin=True, last=True)

        def prepared(u, here):
            return u + AHEAD + here if not isinstance(u, int) else min(u + AHEAD + here, PIECES)

        @block.sync
        def _(sp):
            x_v = x.rearrange("b (n p) d -> p (b n) d", p=P)
            sp.dma_start(x_all[:, 0:CB, :], x_v[:, 0:CB, :]).then_inc(S["x_loaded0"], 16)
            sp.dma_start(wrep[:, :], wqkv.rearrange("(a e) f -> a e f", a=1).to_broadcast([H, HE, 3 * HE]))\
                .then_inc(S["wrep_loaded"], 16)
            for b in range(1, B):
                sp.dma_start(x_all[:, CB * b:CB * (b + 1), :], x_v[:, CB * b:CB * (b + 1), :])\
                    .then_inc(S[f"x_loaded{b}"], 16)

            def store_split(p):
                tok = P * piece_block(p)
                for side in range(2):
                    wait_apart(sp, S["qk_low"], 2 * p + side + 1)
                    for c in range(NP3):
                        rows = split_dram[0, :, :, :, c, bass.ds(tok, PT)] if side == 0 else \
                            split_dram[1, :, :, c, :, bass.ds(tok, PT)]
                        sp.dma_start(rows.rearrange("h f c t -> (h f) c t"), qk_p[:, side, :, :])\
                            .then_inc(S["split_stored"], 16)

            def load_operands(half, u, par, stored):
                wait_apart(sp, S["split_stored"], 16 * 2 * NP3 * stored)
                tok, head = C * step_batch(u) + PT * half, step_head(u, par)
                done = S[f"upper_loaded{par}"] if half else S[f"lower_loaded{par}"]
                for side, op in enumerate((q_op, k_op)):
                    rows = split_dram[side, bass.ds(head, G), :, :, :, bass.ds(tok, PT)]
                    sp.dma_start(op[0:ROWS, par, :, half * PT:(half + 1) * PT],
                                 rows.rearrange("h f a b t -> (f a b) h t")).then_inc(done, 16)

            def load_rows(par, half, t):
                sp.wait_ge(S["rows_copied"], 2 * t + (1 if half else 2))
                sp.dma_start(q_op[MROW:MROW + NP3, par, :, half * PT:(half + 1) * PT], top_t[:, half, :])\
                    .then_inc(S["rows_loaded"], 16)

            out_v = out.rearrange("b (n p) d -> p (b n) d", p=P)

            def store_out(p):
                wait_apart(sp, S["y3_done"], p + 1)
                sp.dma_start(out_v[:, bass.ds(piece_block(p), PB), :], y3[:, :, :]).then_inc(S["stored"], 16)

            def pair(u, prep=False, fin=False, first=False, last=False):
                for par in range(2):
                    t = 2 * u + par
                    for what, *of in ORDER[par]:
                        if what == "READ" and of[0] == "rows" and not (of[2] and last and par):
                            load_rows((par + of[2]) % 2, of[1], t + of[2])
                        elif what == "PREPARE" and of[0] == "split" and prep:
                            store_split(u + AHEAD)
                        elif what == "FINISH" and of[0] == "read y" and fin:
                            store_out(u - AHEAD)
                        elif what == "LOAD" and not last:
                            wait_apart(sp, S["st_full"], NAU * t + (AHALF1 if of[0] else NAU))
                            wait_apart(sp, S["s_full"], NSU * (t + 1))
                            load_operands(of[0], u + 1, par, prepared(u, 1 if prep else 0))

            sp.wait_ge(S["pool_const"], 4)
            for p in range(AHEAD):
                store_split(p)
            for par in range(2):
                for half in (1, 0):
                    load_operands(half, 0, par, AHEAD)
            load_rows(0, 1, 0)
            run(sp, pair)
            for p in range(PIECES - AHEAD, PIECES):
                store_out(p)
            sp.wait_ge(S["stored"], 16 * PIECES)

        @block.scalar
        def _(act):
            for dst, src in (
                (bqk[:, 0:1], bqkv[0:HE].rearrange("(a e f) -> a e f", a=1, f=1).to_broadcast([H, HE, 1])),
                (bqk[:, 1:2], bqkv[HE:2 * HE].rearrange("(a e f) -> a e f", a=1, f=1).to_broadcast([H, HE, 1])),
                (bv[:, :], bqkv[2 * HE:].rearrange("(a b e) -> a b e", a=1, b=1).to_broadcast([P, H, HE])),
                (wr_sb[:, :], wr),
                (br_sb[:, :], br.rearrange("(a d) -> a d", a=1).to_broadcast([P, D])),
                (wf_raw[:, :], wffn),
                (bf_sb[:, :], bffn.rearrange("(a d) -> a d", a=1).to_broadcast([P, D])),
                (isc[:, :], iscale.rearrange("(a d) -> a d", a=1).to_broadcast([P, 1])),
                (wsc[:, :], wscale.rearrange("(a d) -> a d", a=1).to_broadcast([P, 1])),
            ):
                act.dma_start(dst, src).then_inc(S["weights_loaded"], 16)

            act.wait_ge(S["norm_ready"], 1)
            act.activation(std[:, :], vareps[:, :], ACT.Sqrt).then_inc(S["sqrt_done"], 1)
            act.wait_ge(S["wf_full"], 1)
            act.activation(wf_t[:, :], mix_ps[:, 0:P], ACT.Copy).then_inc(S["wf_ready"], 1)
            act.wait_ge(S["weights_loaded"], 144)

            def prepare(stage, p, first=False):
                if stage == "read xt":
                    act.wait_ge(S["xt_full"], p + 1)
                    if not first:
                        act.wait_ge(S["v_full"], p)
                        act.wait_ge(S["scanned"], p)
                        act.wait_ge(S["xs_done"], p)
                    act.activation(xn_t[:, :], mix_ps[:, :], ACT.Copy).then_inc(S["xt_copied"], 1)
                elif stage in ("read q", "read k"):
                    side = int(stage == "read k")
                    act.wait_ge(S["qk_full"], 2 * p + side + 1)
                    if not first:
                        act.wait_ge(S["split_stored"], 16 * 2 * NP3 * p)
                    act.activation(qk_p[:, side, 0, :], mix_ps[:, :], ACT.Identity,
                                   bias=bqk[:, side:side + 1]).then_inc(S["qk_hi"], 1)
                elif stage == "read v":
                    act.wait_ge(S["v_done"], p + 1)
                    act.activation(v_all[:, bass.ds(piece_block(p), PB), :, 0:HE],
                                   v_p[:, :, :].rearrange("p n (h e) -> p n h e", e=HE), ACT.Copy)\
                        .then_inc(S["v_copied"], 1)
                elif stage == "read suf":
                    act.wait_ge(S["suf_full"], p + 1)
                    act.activation(num[:, bass.ds(piece_block(p), PB), :, 0:HE],
                                   mix_ps[:, :].rearrange("p (n h e) -> p n h e", n=PB, e=HE), ACT.Copy)\
                        .then_inc(S["suf_done"], 1)
                elif stage == "read ffn":
                    act.wait_ge(S["z_done"], p + 1)
                    if not first:
                        act.wait_ge(S["sig_done"], p)
                    act.activation(th[:, :, :], z[:, :, :], ACT.Tanh, scale=0.5).then_inc(S["th_done"], 1)

            def diag_copy(n, t, first=False):
                k = sum(v[0] for v in SU[:n])
                act.wait_ge(S["s_full"], NSU * t + n + 1)
                if k >= 4 or not first:
                    act.wait_ge(S["diag_reduced"], 4 * t + k // 2 - 1)
                act.activation(diag[:, k // 2 % 2, k % 2, :, :],
                               s_ps[:, n % 2, :].rearrange("p (h k) -> p h k", h=G), ACT.Copy)\
                    .then_inc(S["diag_copied"], 1)

            def weights0(half, par, t):
                act.wait_ge(S["top_ready"], 2 * t + (1 if half else 2))
                act.activation(e0[:, par, half, :, :], top[:, half, :, :], ACT.Exp, scale=-SCALE)\
                    .then_inc(S["e0_ready"], 1)

            def rows_copy(half, t):
                act.wait_ge(S["rows_full"], 2 * t + (1 if half else 2))
                if not (isinstance(t, int) and t == 0):
                    act.wait_ge(S["rows_loaded"], 16 * (2 * t - (1 if half else 0)))
                act.activation(top_t[:, half, :], mixb_ps[0:NP3 * G, 0:PT], ACT.Copy)\
                    .then_inc(S["rows_copied"], 1)

            def exps(n, t, first):
                half, kb, heads, q0, nq = AU[n]
                act.wait_ge(S["st_full"], NAU * t + n + 1)
                if not (first and n < RING):
                    m, back = (n - RING, 0) if n >= RING else (n - RING + NAU, 1)
                    act.wait_ge(S["pv_done"], NPV * (t - back) + PV_OF[m] + 1)
                w = len(heads) // 2 * nq
                act.activation(probs[:, n % RING, :].rearrange("p (a c) -> p a c", a=2)[:, :, 0:w],
                               st_ps[:, n % 2, :, 0:w], ACT.Exp, scale=SCALE).then_inc(S["exp_done"], 1)

            def pair(u, prep=False, fin=False, first=False, last=False):
                for par in range(2):
                    t = 2 * u + par
                    over = last and par == 1
                    for what, *of in ORDER[par]:
                        if what == "AU":
                            exps(of[0], t, first and par == 0)
                        elif what == "SU" and not over and SU[of[0]][0]:
                            diag_copy(of[0], t + 1)
                        elif what == "MAX" and not (of[1] and over):
                            weights0(of[0], (par + of[1]) % 2, t + of[1])
                        elif what == "READ" and of[0] == "rows" and not (of[2] and over):
                            rows_copy(of[1], t + of[2])
                        elif what == "SUMS":
                            half, = of
                            act.wait_ge(S["pv_done"], NPV * t + (8 if half else NPV))
                            if not (first and par == 0):
                                act.wait_ge(S["sums_full"], 2 * t - (1 if half else 0))
                            act.activation(sums_t[:, half, :], pv_ps[:, :], ACT.Copy).then_inc(S["sums_copied"], 1)
                        elif what == "PREPARE" and prep:
                            prepare(of[0], u + AHEAD)
                        elif what == "FINISH" and fin:
                            finish(of[0], u - AHEAD)

            def finish(stage, p):
                if stage == "read ot":
                    act.wait_ge(S["ot_full"], p + 1)
                    act.activation(o_t[:, :], mix_ps[:, :], ACT.Copy).then_inc(S["ot_copied"], 1)

            for p in range(AHEAD):
                for stage in PREPARE_ALL:
                    prepare(stage, p, p == 0)
            for n in range(NSU):
                if SU[n][0]:
                    diag_copy(n, 0, True)
                if n + 1 == HALF1:
                    weights0(1, 0, 0)
            rows_copy(1, 0)
            run(act, pair)
            for p in range(PIECES - AHEAD, PIECES):
                for stage in FINISH_ALL:
                    finish(stage, p)

        @block.tensor
        def _(pe):
            pe.wait_ge(S["pool_const"], 4)
            pe.wait_ge(S["wf_scaled"], 1)
            pe.transpose(mix_ps[:, 0:P], wf_dq[:, :], ident[:, :]).then_inc(S["wf_full"], 1)
            pe.wait_ge(S["wbd_ready"], 6)
            pe.wait_ge(S["wf_ready"], 1)

            def quarters(product, done):
                for i in range(PB):
                    mm = product(mix_ps[:, P * i:P * (i + 1)], i)
                mm.then_inc(S[done], 1)

            def times(w, operand):
                return lambda to, i: pe.matmul(to, operand[:, P * i:P * (i + 1)], w, start=True, stop=True)

            def fill(kind, n, t=None):
                if kind == "xt":
                    pe.wait_ge(S["xn_ready"], PB * n + PB)
                    quarters(lambda to, i: pe.transpose(to, xn[:, i, :], ident[:, :]), "xt_full")
                    return S["xt_copied"], n + 1
                if kind in ("q", "k"):
                    side = int(kind == "k")
                    pe.wait_ge(S["xt_copied"], n + 1)
                    pe.matmul(mix_ps[:, :], wbd[:, side, :], xn_t[:, :], start=True, stop=True)\
                        .then_inc(S["qk_full"], 1)
                    return S["qk_float"], 2 * n + side + 1
                if kind == "v":
                    quarters(times(wbd[:, 2, :], xn_t), "v_full")
                    return S["v_done"], n + 1
                if kind == "vt":
                    pe.wait_ge(S["v_done"], n + 1)
                    quarters(lambda to, i: pe.transpose(to, v_p[:, i, :], ident[:, :]), "vt_full")
                    return S["scanned"], n + 1
                if kind == "suf":
                    pe.wait_ge(S["scanned"], n + 1)
                    quarters(lambda to, i: pe.transpose(to, suf_t[:, P * i:P * (i + 1)], ident[:, :]), "suf_full")
                    return S["suf_done"], n + 1
                if kind == "ffn":
                    pe.wait_ge(S["xdq_done"], n + 1)
                    quarters(times(wf_t[:, :], x_dq), "ffn_full")
                    return S["z_done"], n + 1
                if kind == "ot":
                    pe.wait_ge(S["o_done"], n + 1)
                    quarters(lambda to, i: pe.transpose(to, o_p[:, i, :], ident[:, :]), "ot_full")
                    return S["ot_copied"], n + 1
                if kind == "y":
                    pe.wait_ge(S["ot_copied"], n + 1)
                    quarters(times(wr_sb[:, :], o_t), "y_full")
                    return S["y1_done"], n + 1
                if kind == "rows":
                    half = n
                    pe.wait_ge(S["low_ready"], 2 * t + (1 if half else 2))
                    for i in range(4):
                        mm = pe.transpose(mixb_ps[0:NP3 * G, P * i:P * (i + 1)], top_p[:, half, i, :, :],
                                          identb[:, :])
                    mm.then_inc(S["rows_full"], 1)
                    return S["rows_copied"], 2 * t + (1 if half else 2)
                half = n
                pe.wait_ge(S["sums_copied"], 2 * t + (1 if half else 2))
                quarters(lambda to, i: pe.transpose(to, sums_t[:, half, P * i:P * (i + 1)], ident[:, :]), "sums_full")
                return S["num_done"], 2 * t + (1 if half else 2)

            def scores(n, u, par, first=False):
                t = 2 * u + par
                is_diag, i, heads, k0, nk = SU[n]
                if n == 0:
                    pe.wait_ge(S[f"upper_loaded{par}"], 32 * (u + 1))
                if n == LOWER:
                    pe.wait_ge(S[f"lower_loaded{par}"], 32 * (u + 1))
                if not (first and n < 2):
                    m, back = (n - 2, 0) if n >= 2 else (n - 2 + NSU, 1)
                    before = sum(v[0] == SU[m][0] for v in SU[:m]) + 1
                    if SU[m][0]:
                        pe.wait_ge(S["diag_copied"], NSD * (t - back) + before)
                    else:
                        pe.wait_ge(S["s_reduced"], NSR * (t - back) + before)
                w = nk * P
                for c, h in enumerate(heads):
                    mm = pe.matmul(s_ps[:, n % 2, c * w:(c + 1) * w], q_op[0:MROW, par, h, P * i:P * (i + 1)],
                                   k_op[0:MROW, par, h, P * k0:P * (k0 + nk)], start=True, stop=True)
                mm.then_inc(S["s_full"], 1)

            def attend(n, par, t, first):
                half, kb, heads, q0, nq = AU[n]
                if not (first and n < 2):
                    pe.wait_ge(S["exp_done"], NAU * t + n - 1)
                if n == 0 or AU[n - 1][0] != half:
                    pe.wait_ge(S["rows_loaded"], 32 * t + (16 if half else 32))
                per = len(heads) // 2
                for c, h in enumerate(heads):
                    mm = pe.matmul(st_ps[:, n % 2, c // per, c % per * nq:(c % per + 1) * nq],
                                   k_op[:, par, h, P * kb:P * (kb + 1)], q_op[:, par, h, q0:q0 + nq],
                                   start=True, stop=True)
                mm.then_inc(S["st_full"], 1)

            def values(m, par, t, first):
                half, kb = PV[m]
                pe.wait_ge(S["exp_done"], NAU * t + PV_UNITS[m][-1] + 1)
                if PV_UNITS[m][-1] in MASKED:
                    pe.wait_ge(S["masked"], NMASK * t + MASKED.index(PV_UNITS[m][-1]) + 1)
                if m == 0:
                    pe.wait_ge(S["v_op_ready"], t + 1)
                if kb == 0 and not (first and half):
                    pe.wait_ge(S["sums_copied"], 2 * t + (0 if half else 1))
                for n in PV_UNITS[m]:
                    _, _, heads, q0, nq = AU[n]
                    per = len(heads) // 2
                    tile = probs[:, n % RING, :].rearrange("p (a c) -> p a c", a=2)
                    for c, h in enumerate(heads):
                        mm = pe.matmul(pv_ps[32 * h:32 * (h + 1), q0 - half * PT:q0 - half * PT + nq],
                                       v_op[:, par, kb, h, :],
                                       tile[:, c // per, c % per * nq:(c % per + 1) * nq],
                                       start=(kb == 0), stop=(kb == 4 * half + 3), skip_group_check=True)
                mm.then_inc(S["pv_done"], 1)

            def pair(u, prep=False, fin=False, first=False, last=False):
                read = (S["rows_copied"], 4 * u + 1)
                for par in range(2):
                    t = 2 * u + par
                    over = last and par == 1
                    for what, *of in ORDER[par]:
                        if what == "AU":
                            attend(of[0], par, t, first and par == 0)
                        elif what == "PV":
                            values(of[0], par, t, first and par == 0)
                        elif what == "SU" and not over:
                            scores(of[0], u + par, 1 - par)
                        elif what == "FILL" and not (of[0] == "rows" and of[2] and over):
                            pe.wait_ge(*read)
                            read = fill(of[0], of[1], t + of[2] if of[0] == "rows" else t)
                        elif what == "PREPARE" and prep and of[0].startswith("fill"):
                            pe.wait_ge(*read)
                            read = fill(of[0].split()[1], u + AHEAD)
                        elif what == "FINISH" and fin and of[0].startswith("fill"):
                            pe.wait_ge(*read)
                            read = fill(of[0].split()[1], u - AHEAD)

            read = (S["wf_ready"], 1)
            for p in range(AHEAD):
                for stage in PREPARE_ALL:
                    if stage.startswith("fill"):
                        pe.wait_ge(*read)
                        read = fill(stage.split()[1], p)
            pe.wait_ge(*read)
            for n in range(NSU):
                scores(n, 0, 0, True)
            fill("rows", 1, 0)
            run(pe, pair)
            read = (S["num_done"], 2 * STEPS)
            for p in range(PIECES - AHEAD, PIECES):
                for stage in FINISH_ALL:
                    if stage.startswith("fill"):
                        pe.wait_ge(*read)
                        read = fill(stage.split()[1], p)

        @block.vector
        def _(dve):
            dve.memset(v_all[:, :, :, HE:VC], 1.0).then_inc(S["setup_dve"], 1)
            dve.memset(carry[:, :], 0.0).then_inc(S["setup_dve"], 1)
            dve.memset(tops[:, :, :, :, :], 0.0).then_inc(S["setup_dve"], 1)
            dve.memset(v_op[:, :, :, :, :], 0.0).then_inc(S["setup_dve"], 1)
            for n in range(NBLK):
                if n % CB == 0:
                    dve.wait_ge(S[f"x_loaded{n // CB}"], 16)
                dve.bn_stats(stats[:, n, :], x_all[:, n, :]).then_inc(S["stats_done"], 1)
            dve.wait_ge(S["stats_done"], NBLK)
            dve.tensor_tensor(mean2[:, :], stats[:, :, 1], stats[:, :, 4], ALU.add).then_inc(S["mean_done"], 1)
            dve.tensor_tensor(dev[:, :], stats[:, :, 1], stats[:, :, 4], ALU.subtract).then_inc(S["mean_done"], 1)
            dve.tensor_tensor(m2[:, :], stats[:, :, 2], stats[:, :, 5], ALU.add).then_inc(S["mean_done"], 1)
            dve.wait_ge(S["mean_done"], 3)
            dve.tensor_scalar(mean[:, :], mean2[:, :], 0.5, None, ALU.mult).then_inc(S["mean_done"], 1)
            dve.tensor_tensor(dev2[:, :], dev[:, :], dev[:, :], ALU.mult).then_inc(S["mean_done"], 1)
            dve.wait_ge(S["mean_done"], 5)
            dve.scalar_tensor_tensor(out=var[:, :], in0=dev2[:, :], scalar=D / 4.0, in1=m2[:, :], op0=ALU.mult,
                                     op1=ALU.add).then_inc(S["mean_done"], 1)
            dve.wait_ge(S["mean_done"], 6)
            dve.tensor_scalar(vareps[:, :], var[:, :], 1.0 / D, EPS, ALU.mult, ALU.add).then_inc(S["norm_ready"], 1)
            dve.wait_ge(S["sqrt_done"], 1)
            dve.reciprocal(rstd[:, :], std[:, :]).then_inc(S["mean_done"], 1)
            dve.wait_ge(S["weights_loaded"], 144)
            dve.tensor_scalar(wf_dq[:, :], wf_raw[:, :], wsc[:, 0:1], None, ALU.mult).then_inc(S["wf_scaled"], 1)
            dve.reciprocal(risc[:, :], isc[:, :]).then_inc(S["mean_done"], 1)
            dve.wait_ge(S["pool_const"], 5)
            dve.tensor_copy(count[:, :], count_i[:, :]).then_inc(S["mean_done"], 1)
            dve.wait_ge(S["mean_done"], 9)
            for b in range(B):
                dve.tensor_copy(num[:, CB * b:CB * (b + 1), :, HE],
                                count[:, :].rearrange("p (n a) -> p n a", a=1).to_broadcast([P, CB, H]))\
                    .then_inc(S["setup_dve"], 1)

            def prepare(stage, p, first=False):
                if stage == "norm":
                    blk = piece_block(p)
                    if not first:
                        dve.wait_ge(S["xt_full"], p)
                    for i in range(PB):
                        dve.tensor_scalar(xn[:, i, :], x_all[:, bass.ds(blk + i, 1), :],
                                          mean[:, bass.ds(blk + i, 1)], rstd[:, bass.ds(blk + i, 1)],
                                          ALU.subtract, ALU.mult).then_inc(S["xn_ready"], 1)
                elif stage in ("read q", "read k"):
                    side = int(stage == "read k")
                    if not first:
                        dve.wait_ge(S["qk_res"], 2 * p)
                    dve.wait_ge(S["qk_hi"], 2 * p + side + 1)
                    dve.tensor_scalar(qk_f[:, side, :], mix_ps[:, :], bqk[:, side:side + 1], None, ALU.add)\
                        .then_inc(S["qk_float"], 1)
                elif stage == "read v":
                    dve.wait_ge(S["v_full"], p + 1)
                    if not first:
                        dve.wait_ge(S["v_copied"], p)
                    dve.tensor_tensor(v_p[:, :, :], mix_ps[:, :].rearrange("p (n d) -> p n d", n=PB),
                                      bv[:, :].rearrange("p (a d) -> p a d", a=1).to_broadcast([P, PB, D]), ALU.add)\
                        .then_inc(S["v_done"], 1)
                elif stage == "read vt":
                    dve.wait_ge(S["vt_full"], p + 1)
                    if not first:
                        dve.wait_ge(S["suf_full"], p)
                        dve.wait_ge(S["carry_done"], p)
                    else:
                        dve.wait_ge(S["setup_dve"], 4 + B)
                    dve.tensor_tensor_scan(suf_t[:, ::-1], mix_ps[:, ::-1], xn_t[:, :],
                                           carry[:, bass.ds(piece_carry(p), 1)], ALU.add, ALU.bypass)\
                        .then_inc(S["scanned"], 1)
                    dve.wait_ge(S["scanned"], p + 1)
                    dve.tensor_copy(carry[:, bass.ds(piece_carry(p) + 1, 1)],
                                    suf_t[:, 0:1]).then_inc(S["carry_done"], 1)
                elif stage == "quantise":
                    dve.wait_ge(S["xt_copied"], p + 1)
                    if not first:
                        dve.wait_ge(S["fine_done"], p)
                        dve.wait_ge(S["half_done"], p)
                    dve.tensor_scalar(xs[:, :], xn_t[:, :], risc[:, 0:1], None, ALU.mult).then_inc(S["xs_done"], 1)
                    dve.wait_ge(S["xs_done"], p + 1)
                    dve.tensor_scalar(xs_half[:, :], xs[:, :], 0.5, None, ALU.mult).then_inc(S["half_done"], 1)
                    if not first:
                        wait_apart(dve, S["far_done"], p)
                        wait_apart(dve, S["xq_done"], p)
                    dve.tensor_scalar(x_fine[:, :], xs[:, :], FINE, -FINE, ALU.min, ALU.max, saturate=False)\
                        .then_inc(S["fine_done"], 1)
                    wait_apart(dve, S["half_done"], p + 1)
                    dve.tensor_scalar(x_pos[:, :], xs_half[:, :], FINE / 2, FP8_MAX / 2, ALU.max, ALU.min,
                                      saturate=False).then_inc(S["pos_done"], 1)
                    dve.tensor_scalar(x_neg[:, :], xs_half[:, :], -FINE / 2, -FP8_MAX / 2, ALU.min, ALU.max,
                                      saturate=False).then_inc(S["neg_done"], 1)
                    wait_apart(dve, S["neg_done"], p + 1)
                    wait_apart(dve, S["pos_done"], p + 1)
                    dve.tensor_tensor(x_far[:, :], x_pos[:, :], x_neg[:, :], ALU.add).then_inc(S["far_done"], 1)
                    wait_apart(dve, S["far_done"], p + 1)
                    wait_apart(dve, S["fine_done"], p + 1)
                    dve.scalar_tensor_tensor(out=x_q[:, :], in0=x_far[:, :], scalar=2.0, in1=x_fine[:, :],
                                             op0=ALU.mult, op1=ALU.add).then_inc(S["xq_done"], 1)
                    dve.wait_ge(S["xq_done"], p + 1)
                    if not first:
                        dve.wait_ge(S["ffn_full"], p)
                    dve.tensor_scalar(x_dq[:, :], x_q[:, :], isc[:, 0:1], None, ALU.mult).then_inc(S["xdq_done"], 1)
                elif stage == "read ffn":
                    dve.wait_ge(S["ffn_full"], p + 1)
                    if not first:
                        dve.wait_ge(S["gate_done"], p)
                    dve.tensor_tensor(z[:, :, :], mix_ps[:, :].rearrange("p (n d) -> p n d", n=PB),
                                      bf_sb[:, :].rearrange("p (a d) -> p a d", a=1).to_broadcast([P, PB, D]),
                                      ALU.add).then_inc(S["z_done"], 1)
                    dve.wait_ge(S["th_done"], p + 1)
                    dve.tensor_scalar(sig[:, :, :], th[:, :, :], 0.5, 0.5, ALU.mult, ALU.add)\
                        .then_inc(S["sig_done"], 1)

            def finish(stage, p, first=False, steps=None):
                if stage == "divide":
                    dve.wait_ge(S["num_done"], steps)
                    if not first:
                        dve.wait_ge(S["o_done"], p)
                    dve.reciprocal(rden[:, :, :], num[:, bass.ds(piece_block(p), PB), :, HE])\
                        .then_inc(S["den_inverted"], 1)
                elif stage == "read y":
                    dve.wait_ge(S["y_full"], p + 1)
                    if not first:
                        dve.wait_ge(S["y2_done"], p)
                    dve.tensor_tensor(y1[:, :, :], mix_ps[:, :].rearrange("p (n d) -> p n d", n=PB),
                                      br_sb[:, :].rearrange("p (a d) -> p a d", a=1).to_broadcast([P, PB, D]),
                                      ALU.add).then_inc(S["y1_done"], 1)

            def reduce(n, t):
                is_diag, i, heads, k0, nk = SU[n]
                half = i // 4
                if is_diag:
                    return
                r = n - sum(v[0] for v in SU[:n])
                dve.wait_ge(S["s_full"], NSU * t + n + 1)
                slot = 0 if k0 == 0 else 1
                dve.tensor_reduce(tops[:, half, i % 4, heads[0]:heads[-1] + 1, slot],
                                  s_ps[:, n % 2, 0:len(heads) * nk * P].rearrange("p (h k) -> p h k", h=len(heads)),
                                  AX.X, ALU.max).then_inc(S["s_reduced"], 1)

            def reduce_diag(k, t):
                half, i = (1, 0) if k < 2 else (0, 0)
                i = 2 * (k % 2)
                dve.wait_ge(S["diag_masked"], 4 * t + k + 1)
                dve.tensor_reduce(tops[:, half, i:i + 2, :, 2],
                                  diag[:, k % 2, :, :, :], AX.X, ALU.max).then_inc(S["diag_reduced"], 1)

            def maxima(half, t, first=False):
                n = 2 * t + (1 if half else 2)
                dve.wait_ge(S["s_reduced"], NSR * t + (HALF1_R if half else NSR))
                dve.wait_ge(S["diag_reduced"], 4 * t + (2 if half else 4))
                if not first:
                    dve.wait_ge(S["e0_ready"], n - 2)
                    dve.wait_ge(S["rows_full"], n - 2)
                dve.tensor_reduce(top[:, half, :, :], tops[:, half, :, :, :], AX.X, ALU.max)\
                    .then_inc(S["top_ready"], 1)
                dve.wait_ge(S["top_ready"], n)
                dve.tensor_scalar(top_p[:, half, :, 0, :], top[:, half, :, :], -1.0, None, ALU.mult)\
                    .then_inc(S["hi_ready"], 1)
                dve.wait_ge(S["hi_ready"], n)
                dve.scalar_tensor_tensor(out=top_r[:, half, :, :], in0=top[:, half, :, :], scalar=-1.0,
                                         in1=top_p[:, half, :, 0, :], op0=ALU.mult, op1=ALU.subtract)\
                    .then_inc(S["res_ready"], 1)
                dve.wait_ge(S["res_ready"], n)
                dve.tensor_copy(top_p[:, half, :, 1, :], top_r[:, half, :, :]).then_inc(S["mid_ready"], 1)
                dve.wait_ge(S["mid_ready"], n)
                dve.tensor_tensor(top_p[:, half, :, 2, :], top_r[:, half, :, :], top_p[:, half, :, 1, :], ALU.subtract)\
                    .then_inc(S["low_ready"], 1)

            def gather(half, u, par, first):
                t = 2 * u + par
                n = 2 * t + (1 if half else 2)
                mine = num[:, bass.ds(CB * step_batch(u) + 4 * half, 4), bass.ds(step_head(u, par), G), :]
                dve.wait_ge(S["e0_ready"], n)
                dve.wait_ge(S["suf_done"], prepared(u, 0))
                if not first:
                    dve.wait_ge(S["num_done"], n - 2)
                dve.tensor_tensor(scaled[:, half, :, :, :], mine,
                                  e0[:, par, half, :, :].rearrange("p i (h a) -> p i h a", a=1)
                                  .to_broadcast([P, 4, G, VC]), ALU.mult).then_inc(S["scaled_done"], 1)
                dve.wait_ge(S["sums_full"], n)
                dve.wait_ge(S["scaled_done"], n)
                dve.tensor_tensor(mine, scaled[:, half, :, :, :],
                                  mix_ps[:, :].rearrange("p (i h c) -> p i h c", i=4, h=G)[:, :, :, 0:VC],
                                  ALU.add).then_inc(S["num_done"], 1)

            def pair(u, prep=False, fin=False, first=False, last=False):
                for par in range(2):
                    t = 2 * u + par
                    over = last and par == 1
                    for what, *of in ORDER[par]:
                        if what == "SU" and not over:
                            reduce(of[0], t + 1)
                            if of[0] in DIAG_AFTER:
                                reduce_diag(DIAG_AFTER[of[0]], t + 1)
                        elif what == "MAX" and not (of[1] and over):
                            maxima(of[0], t + of[1], first and par == 0 and not of[1])
                        elif what == "READ" and of[0] == "out":
                            gather(of[1], u, par, first and par == 0)
                        elif what == "PREPARE" and prep:
                            prepare(of[0], u + AHEAD)
                        elif what == "FINISH" and fin:
                            finish(of[0], u - AHEAD, isinstance(u, int) and u == AHEAD, 4 * u)

            for p in range(AHEAD):
                for stage in PREPARE_ALL:
                    prepare(stage, p, p == 0)
            for n in range(NSU):
                reduce(n, 0)
                if n in DIAG_AFTER:
                    reduce_diag(DIAG_AFTER[n], 0)
                if n + 1 == HALF1:
                    maxima(1, 0, True)
            run(dve, pair)
            for p in range(PIECES - AHEAD, PIECES):
                for stage in FINISH_ALL:
                    finish(stage, p, False, 2 * STEPS)

        @block.gpsimd
        def _(pool):
            pool.memset(ident[:, :], 0.0).then_inc(S["pool_const"], 1)
            pool.wait_ge(S["pool_const"], 1)
            pool.affine_select(out=ident[:, :], in_=ident[:, :], compare_op=ALU.not_equal, fill=1.0, base=0,
                               pattern=[[-1, P]], channel_multiplier=1).then_inc(S["pool_const"], 1)
            pool.wait_ge(S["pool_const"], 2)
            pool.tensor_copy(identb[:, :], ident[:, :]).then_inc(S["pool_const"], 1)
            pool.wait_ge(S["pool_const"], 3)
            pool.memset(q_op[64:128, :, :, :].bitcast(F32), 0.0).then_inc(S["rows_set"], 1)
            pool.wait_ge(S["rows_set"], 1)
            pool.memset(k_op[64:128, :, :, :].bitcast(F32), 0.0).then_inc(S["rows_set"], 1)
            pool.wait_ge(S["rows_set"], 2)
            pool.memset(k_op[MROW:MROW + NP3, :, :, :], 1.0).then_inc(S["pool_const"], 1)
            pool.wait_ge(S["pool_const"], 4)
            pool.iota(count_i[:, :], pattern=[[-P, CB]], base=C, channel_multiplier=-1)\
                .then_inc(S["pool_const"], 1)
            pool.wait_ge(S["wrep_loaded"], 16)
            for m in range(3):
                src = wrep[:, HE * m:HE * (m + 1)].rearrange("p (a f) -> p a f", a=1).to_broadcast([P, H, HE])
                pool.affine_select(out=wbd_half[:, m, :].rearrange("p (h f) -> p h f", h=H), in_=src,
                                   compare_op=ALU.is_ge, fill=0.0, base=0, pattern=[[-HE, H], [0, HE]],
                                   channel_multiplier=1).then_inc(S["wbd_ready"], 1)
            pool.wait_ge(S["wbd_ready"], 3)
            for m in range(3):
                last = pool.affine_select(out=wbd[:, m, :].rearrange("p (h f) -> p h f", h=H),
                                          in_=wbd_half[:, m, :].rearrange("p (h f) -> p h f", h=H),
                                          compare_op=ALU.is_ge, fill=0.0, base=HE - 1,
                                          pattern=[[HE, H], [0, HE]], channel_multiplier=-1)
                last.then_inc(S["wbd_ready"], 1)
            pool.wait_ge(S["weights_loaded"], 144)

            def prepare(stage, p, first=False):
                if stage in ("read q", "read k"):
                    side = int(stage == "read k")
                    n = 2 * p + side + 1
                    pool.wait_ge(S["qk_float"], n)
                    pool.wait_ge(S["qk_hi"], n)
                    pool.tensor_tensor(qk_p[:, side, 1, :], qk_f[:, side, :], qk_p[:, side, 0, :], ALU.subtract)\
                        .then_inc(S["qk_mid"], 1)
                    if not first:
                        pool.wait_ge(S["qk_low"], n - 2)
                    pool.tensor_tensor(qk_r[:, side, :], qk_f[:, side, :], qk_p[:, side, 0, :], ALU.subtract)\
                        .then_inc(S["qk_res"], 1)
                    pool.wait_ge(S["qk_mid"], n)
                    pool.wait_ge(S["qk_res"], n)
                    pool.tensor_tensor(qk_p[:, side, 2, :], qk_r[:, side, :], qk_p[:, side, 1, :], ALU.subtract)\
                        .then_inc(S["qk_low"], 1)
                elif stage == "read ffn":
                    pool.wait_ge(S["sig_done"], p + 1)
                    pool.tensor_tensor(gate[:, bass.ds(piece_block(p), PB), :], z[:, :, :], sig[:, :, :], ALU.mult)\
                        .then_inc(S["gate_done"], 1)

            def finish(stage, p, first=False):
                if stage == "divide":
                    mine = num[:, bass.ds(piece_block(p), PB), :, :]
                    if not first:
                        pool.wait_ge(S["ot_full"], p)
                    pool.wait_ge(S["den_inverted"], p + 1)
                    pool.tensor_tensor(o_p[:, :, :].rearrange("p n (h e) -> p n h e", e=HE), mine[:, :, :, 0:HE],
                                       rden[:, :, :].rearrange("p n (h a) -> p n h a", a=1)
                                       .to_broadcast([P, PB, H, HE]), ALU.mult).then_inc(S["o_done"], 1)
                elif stage == "read y":
                    blk = piece_block(p)
                    pool.wait_ge(S["y1_done"], p + 1)
                    pool.wait_ge(S["gate_done"], p + 1)
                    if not first:
                        pool.wait_ge(S["y3_done"], p)
                    pool.tensor_tensor(y2[:, :, :], y1[:, :, :], gate[:, bass.ds(blk, PB), :], ALU.mult)\
                        .then_inc(S["y2_done"], 1)
                    pool.wait_ge(S["y2_done"], p + 1)
                    if not first:
                        pool.wait_ge(S["stored"], 16 * p)
                    pool.tensor_tensor(y3[:, :, :], y2[:, :, :], x_all[:, bass.ds(blk, PB), :], ALU.add)\
                        .then_inc(S["y3_done"], 1)

            def mask_diag(k, t):
                wait_apart(pool, S["diag_copied"], NSD * t + 2 * k + 2)
                tile = diag[:, k % 2, :, :, :].rearrange("p i h k -> p (i h) k")
                pool.affine_select(out=tile, in_=tile, compare_op=ALU.is_gt, fill=0.0, base=0,
                                   pattern=[[0, 2 * G], [-1, P]], channel_multiplier=1)\
                    .then_inc(S["diag_masked"], 1)

            def load_v(u, par, pieces):
                t = 2 * u + par
                if not (isinstance(t, int) and t < 2):
                    pool.wait_ge(S["pv_done"], NPV * (t - 1))
                pool.wait_ge(S["v_copied"], pieces)
                pool.tensor_copy(v_op[:, par, :, :, 0:VC],
                                 v_all[:, bass.ds(CB * step_batch(u), CB), bass.ds(step_head(u, par), G), :])\
                    .then_inc(S["v_op_ready"], 1)

            def mask_exps(n, t):
                half, kb, heads, q0, nq = AU[n]
                per = len(heads) // 2
                wait_apart(pool, S["exp_done"], NAU * t + n + 1)
                for a in range(2):
                    tile = probs[:, n % RING, a * PT:a * PT + per * nq]\
                        .rearrange("p (c q) -> p c q", c=per)[:, :, 0:P]
                    done = pool.affine_select(out=tile, in_=tile, compare_op=ALU.is_gt, fill=0.0, base=0,
                                              pattern=[[0, per], [1, P]], channel_multiplier=-1)
                done.then_inc(S["masked"], 1)

            def pair(u, prep=False, fin=False, first=False, last=False):
                for par in range(2):
                    t = 2 * u + par
                    over = last and par == 1
                    for what, *of in ORDER[par]:
                        if what == "AU" and of[0] in MASKED:
                            mask_exps(of[0], t)
                        elif what == "SU" and not over and of[0] in MASK_AFTER:
                            mask_diag(MASK_AFTER[of[0]], t + 1)
                        elif what == "LOADV" and not over:
                            load_v(u + par, 1 - par, prepared(u, par if prep else 0))
                        elif what == "PREPARE" and prep:
                            prepare(of[0], u + AHEAD)
                        elif what == "FINISH" and fin:
                            finish(of[0], u - AHEAD, isinstance(u, int) and u == AHEAD)

            for p in range(AHEAD):
                for stage in PREPARE_ALL:
                    prepare(stage, p, p == 0)
            pool.wait_ge(S["setup_dve"], 4)
            load_v(0, 0, AHEAD)
            for n in range(NSU):
                if n in MASK_AFTER:
                    mask_diag(MASK_AFTER[n], 0)
            run(pool, pair)
            for p in range(PIECES - AHEAD, PIECES):
                for stage in FINISH_ALL:
                    finish(stage, p)


_INS = ["L0_attn_x", "L0_attn_Wqkv", "L0_attn_bqkv", "L0_attn_Wr", "L0_attn_br", "L0_ffn_weight_fp8",
        "L0_ffn_bias", "L0_ffn_input_scale", "L0_ffn_weight_scale"]


def kernel(**inputs):
    import concourse.bacc as bacc
    from concourse.bass_utils import run_bass_kernel_spmd

    nc = bacc.Bacc("TRN2", target_bir_lowering=False, num_devices=1)
    arrays, args = {}, []
    for name in _INS:
        a = np.ascontiguousarray(inputs[name])
        arrays[name] = a
        args.append(nc.dram_tensor(name, a.shape, mybir.dt.from_np(a.dtype), kind="ExternalInput").ap())
    args.append(nc.dram_tensor("out", (B, C, D), F32, kind="ExternalOutput").ap())
    program(nc, *args)
    r = run_bass_kernel_spmd(nc, [arrays], core_ids=[0])
    return r.results[0]["out"]
```

```python
from contextlib import ExitStack

import numpy as np

import concourse.bass as bass
from concourse import mybir

F32 = mybir.dt.float32
BF16 = mybir.dt.bfloat16
FP8 = mybir.dt.float8e4
I32 = mybir.dt.int32
ALU = mybir.AluOpType
ACT = mybir.ActivationFunctionType
AX = mybir.AxisListType

P = 128
B, C, D, H = 4, 1024, 128, 16
HE = D // H
TOK = B * C
NBLK = TOK // P
CB = C // P
G = 4
NG = H // G
STEPS = B * NG
PT = 512
PB = PT // P
PIECES = TOK // PT
NP3 = 3
ROWS = NP3 * NP3 * HE
MROW = 96
VC = HE + 1
SCALE = float(1.0 / np.sqrt(np.float32(HE)))
EPS = 1e-5
FP8_MAX = 448.0
TWO_ONES = float(np.array([0x3F803F80], np.uint32).view(np.float32)[0])
FINE = 16.0



KEY_ORDER = (1, 5, 6, 4, 0, 2, 7, 3)
DIAG_GAP = (1, 4)


def score_units():
    units = []
    for half in (1, 0):
        blocks, rest = range(half * 4, half * 4 + 4), []
        for i in reversed(blocks):
            nk, first = i % 4, i - i % 4
            if nk:
                per = 2 if i == 1 else 4 // nk
                rest += [(False, i, tuple(range(h, h + per)), first, nk) for h in range(0, G, per)]
        for i in reversed(blocks):
            if i >= 4:
                rest += [(False, i, (h,), 0, 4) for h in range(G)]
        gap = DIAG_GAP[half]
        for n, i in enumerate(blocks):
            units += [(True, i, (0, 1, 2, 3), i, 1)] + rest[gap * n:gap * (n + 1)]
        units += rest[gap * 4:]
    return units


def attend_units():
    units = []
    for half, kbs in ((1, KEY_ORDER), (0, (0, 1, 2, 3))):
        for kb in kbs:
            q0 = max(half * PT, kb * P)
            n = (half + 1) * PT - q0
            per = 2 if half == 0 and n == P else PT // n
            units += [(half, kb, tuple(range(h, h + per)), q0, n) for h in range(0, G, per)]
    return units


def slot_before(n, slots, units):
    return (n - slots) % units, int(n < slots)


SU = score_units()
AU = attend_units()
NSU, NAU = len(SU), len(AU)
assert NSU == NAU
NSD = sum(u[0] for u in SU)
NSR = NSU - NSD
HALF1 = max(n for n, u in enumerate(SU) if u[1] >= 4) + 1
HALF1_R = sum(not u[0] for u in SU[:HALF1])
LOWER = min(n for n, u in enumerate(SU) if u[3] < 4)
AHALF1 = sum(u[0] for u in AU)
PV = [(1, kb) for kb in KEY_ORDER] + [(0, kb) for kb in range(4)]
NPV = len(PV)
NPV1 = sum(half for half, _ in PV)
PV_UNITS = [[n for n, u in enumerate(AU) if (u[0], u[1]) == pv] for pv in PV]
PV_OF = [PV.index((u[0], u[1])) for u in AU]
MASKED = [n for n, (half, kb, _, q0, _) in enumerate(AU) if q0 == kb * P]
NMASK = len(MASKED)
RING = 13
SBANKS, STBANKS = 3, 3
assert NAU % RING == 0 and NAU % STBANKS == 0 and NSU % SBANKS == 0
PV_AT = (7, 10, 15, 19, 22, 26, 28, 29, 35, 38, 40, 42)
assert all(at > units[-1] for at, units in zip(PV_AT, PV_UNITS))
DIAG_DONE = [n for n, u in enumerate(SU) if u[0]][1::2]
MASK_DELAY = 0
MASK_AFTER = {min(n + MASK_DELAY, (HALF1 if n < HALF1 else NSU) - 1): k for k, n in enumerate(DIAG_DONE)}
DIAG_DELAY = 4
DIAG_AFTER = {min(n + DIAG_DELAY, (HALF1 if n < HALF1 else NSU) - 1): k for k, n in enumerate(DIAG_DONE)}

LAST_FINISH = {35: ["divide", "times"], 36: ["fill ot"], 37: ["read ot"]}
LEFT_FINISH = [("divide", 1), ("times", 1), ("fill y", 0), ("read y", 0), ("fill ot", 1), ("read ot", 1), ("add", 0),
               ("fill y", 1), ("read y", 1), ("add", 1)]

PREPARE = {"norm": 0, "fill xt": 3, "read xt": 4, "fill q": 12, "read q": 13, "mid q": 13, "low q": 15,
           "fill k": 16, "read k": 19, "mid k": 19, "low k": 21, "split": 23, "scale": 23, "near": 26, "far": 29,
           "rescale": 35, "fill v": NAU + 4, "read v": NAU + 5, "fill vt": NAU + 12, "read vt": NAU + 14,
           "fill suf": NAU + 18, "read suf": NAU + 19, "fill ffn": NAU + 20, "read ffn": NAU + 21,
           "gate": NAU + 24, "keep v": NAU + 5, "tanh": NAU + 23}
FINISH = {"divide": NAU + 5, "times": NAU + 17, "fill ot": NAU + 23, "read ot": NAU + 24, "fill y": NAU + 26,
          "read y": NAU + 27, "add": NAU + 27}
AT = {"max 0": 1, "fill out 0": 6, "read out 0": 7, "fill rows 0": 9, "read rows 0": 10, "v": 23,
      "fill rows 1": 29, "read rows 1": 30, "fill out 1": 32, "read out 1": 33, "weight 0": 7, "weight 1": 34,
      "parts 0": 1, "parts 1": 26}


def step_order(parity):
    order = []

    def products(n):
        for back in (1, 0):
            for m in range(NPV):
                if PV_AT[m] == n + back * NAU:
                    order.append((-back, "PV", m))
                    if m + 1 in (NPV1, NPV):
                        order.append((-back, "SUMS", PV[m][0]))

    for n in range(NAU):
        order.append((0, "AU", n))
        order.append((1, "SU", n))
        if n == HALF1 - 1:
            order.append((1, "MAX", 1))
        products(n)
        if n == AT["max 0"]:
            order.append((0, "MAX", 0))
        for half in range(2):
            if n == AT[f"weight {half}"]:
                order.append((half, "WEIGHT", half))
            if n == AT[f"parts {half}"]:
                order.append((half, "PARTS", half))
        for step, what, half in ((0, "rows", 0), (1, "rows", 1), (-1, "out", 0), (0, "out", 1)):
            for kind in ("FILL", "READ"):
                if n == AT[f"{kind.lower()} {what} {half}"]:
                    order.append((step, kind, what, half))
        order += [(0, "PREPARE", stage) for stage, at in PREPARE.items() if at == n + parity * NAU]
        order += [(0, "FINISH", stage) for stage, at in FINISH.items() if at == n + parity * NAU]
        if n == AT["v"]:
            order.append((1, "LOADV"))
        if n == AHALF1:
            order.append((2, "LOAD", 1))
        if n == NAU - 1:
            order.append((2, "LOAD", 0))
    return order


ORDER = [step_order(0), step_order(1)]
assert [e[2:] for e in ORDER[1] if e[1] == "FILL"][-1] == ("out", 1)
PAIRS = STEPS // 2
AHEAD = PIECES // B
SPLIT = 16 * 2 * NP3


def pieces_for(u):
    return min(u + AHEAD, PIECES) if isinstance(u, int) else u + AHEAD


def later(count, least=1):
    return not isinstance(count, int) or count >= least


def later_than_loop(p):
    """Whether a piece is finished after the last pair has begun its last step."""
    return isinstance(p, int) and p >= PIECES - AHEAD


def events(u):
    for par in range(2):
        for step, what, *of in ORDER[par]:
            if what in ("PREPARE", "FINISH"):
                p = u + (AHEAD if what == "PREPARE" else -AHEAD)
                if not isinstance(u, int) or 0 <= p < PIECES:
                    yield what, p, None, of
            else:
                its = u + (par + step) // 2
                if not isinstance(u, int) or 0 <= its < PAIRS:
                    yield what, its, (par + step) % 2, of
            if isinstance(u, int) and u == PAIRS - 1 and par == 1 and what == "AU":
                for stage in LAST_FINISH.get(of[0], ()):
                    yield "FINISH", PIECES - AHEAD, None, [stage]


FIRST = [("PREPARE", "norm", 0), ("SETUP", "measure", 1), ("PREPARE", "fill xt", 0), ("PREPARE", "read xt", 0),
         ("PREPARE", "norm", 1), ("PREPARE", "fill xt", 1), ("PREPARE", "read xt", 1), ("SETUP", "measure", 2),
         ("SETUP", "measure", 3)]
for _p in range(AHEAD):
    for _side in "qk":
        FIRST += [("PREPARE", f"{_stage} {_side}", _p) for _stage in ("fill", "read", "mid", "low")]
    FIRST.append(("PREPARE", "split", _p))
BETWEEN = {("fill v", 0): -1, ("read v", 0): -1, ("scale", 0): -1, ("near", 0): -1, ("fill vt", 0): -1,
           ("read vt", 0): 0, ("keep v", 0): -1, ("far", 0): 4, ("rescale", 0): 5, ("fill suf", 0): 1,
           ("read suf", 0): 2, ("fill ffn", 0): 9, ("read ffn", 0): 10, ("tanh", 0): 12, ("gate", 0): 13,
           ("fill v", 1): 7, ("read v", 1): 8, ("keep v", 1): 9, ("scale", 1): 8, ("near", 1): 27,
           ("fill vt", 1): 11, ("read vt", 1): 12, ("far", 1): 28, ("rescale", 1): 31, ("fill suf", 1): 15,
           ("read suf", 1): 17, ("fill ffn", 1): 32, ("read ffn", 1): 33, ("tanh", 1): 34, ("gate", 1): 36}


def events_ahead():
    for what, stage, p in FIRST:
        yield what, p, None, [stage]
    yield "SETUP", 1, None, ["statistics"]
    yield "SETUP", 0, None, ["weights"]

    def rest(n):
        for (stage, p), at in BETWEEN.items():
            if at == n:
                yield "PREPARE", p, None, [stage]
    yield from rest(-1)
    for step, what, *of in ORDER[1]:
        if step == 1:
            yield what, 0, 0, of
            if what == "SU":
                yield from rest(of[0])


def events_left():
    for step, what, *of in ORDER[0]:
        if step == -1:
            yield what, PAIRS - 1, 1, of
    for stage, which in LEFT_FINISH:
        yield "FINISH", PIECES - AHEAD + which, None, [stage]


def program(nc, x, wqkv, bqkv, wr, br, wffn, bffn, iscale, wscale, out):
    ctx = ExitStack()
    with ctx:
        def sb(name, shape, dt=F32):
            return ctx.enter_context(nc.sbuf_tensor(name, shape, dt))

        def ps(name, shape, dt=F32):
            return ctx.enter_context(nc.psum_tensor(name, shape, dt))

        sems = {}

        def sem(name):
            sems[name] = ctx.enter_context(nc.semaphore(name))
            return sems[name]

        split_dram = nc.dram_tensor("split_dram", (2, H, HE, NP3, NP3, TOK), BF16, kind="Internal").ap()
        x_all = sb("x_all", [P, NBLK, D])
        gate = sb("gate", [P, NBLK, D])
        v_all = sb("v_all", [P, NBLK, H, VC])
        num = sb("num", [P, NBLK, H, VC])
        q_op = sb("q_op", [P, 2, G, C], BF16)
        k_op = sb("k_op", [P, 2, G, C], BF16)
        v_op = sb("v_op", [P, 2, CB, G, 32])
        probs = sb("probs", [P, RING, PT])
        diag = sb("diag", [P, 2, 2, G, P])
        ident = sb("ident", [P, P])
        identb = sb("identb", [P, P], BF16)
        wrep = sb("wrep", [P, 3 * HE])
        wbd = sb("wbd", [P, 3, P])
        wbd_half = sb("wbd_half", [P, 3, P])
        bqk = sb("bqk", [P, 2])
        bv = sb("bv", [P, P])
        wr_sb = sb("wr_sb", [P, D])
        br_sb = sb("br_sb", [P, D])
        wf_raw = sb("wf_raw", [P, D])
        wf_dq = sb("wf_dq", [P, D])
        wf_t = sb("wf_t", [P, D])
        bf_sb = sb("bf_sb", [P, D])
        isc = sb("isc", [P, 1])
        risc = sb("risc", [P, 1])
        wsc = sb("wsc", [P, 1])
        stats = sb("stats", [P, NBLK, 6])
        mean2 = sb("mean2", [P, NBLK])
        mean = sb("mean", [P, NBLK])
        dev = sb("dev", [P, NBLK])
        dev2 = sb("dev2", [P, NBLK])
        m2 = sb("m2", [P, NBLK])
        var = sb("var", [P, NBLK])
        vareps = sb("vareps", [P, NBLK])
        std = sb("std", [P, NBLK])
        rstd = sb("rstd", [P, NBLK])
        count_i = sb("count_i", [P, CB], I32)
        count = sb("count", [P, CB])
        xn = sb("xn", [P, PB, D])
        xn_t = sb("xn_t", [P, PT])
        qk_f = sb("qk_f", [P, 2, PT])
        qk_r = sb("qk_r", [P, 2, PT])
        qk_p = sb("qk_p", [P, 2, NP3, PT], BF16)
        v_p = sb("v_p", [P, PB, D])
        suf_t = sb("suf_t", [P, PT])
        carry = sb("carry", [P, PIECES + B])
        xs = sb("xs", [P, PT])
        xs_half = sb("xs_half", [P, PT])
        x_fine = sb("x_fine", [P, PT], FP8)
        x_pos = sb("x_pos", [P, PT], FP8)
        x_neg = sb("x_neg", [P, PT], FP8)
        x_far = sb("x_far", [P, PT])
        x_q = sb("x_q", [P, PT])
        x_dq = sb("x_dq", [P, PT])
        z = sb("z", [P, PB, D])
        th = sb("th", [P, PB, D])
        tops = sb("tops", [P, 2, 4, G, 3])
        top = sb("top", [P, 2, 4, G])
        e0 = sb("e0", [P, 2, 2, 4, G])
        top_n = sb("top_n", [P, 2, 4, G])
        top_r = sb("top_r", [P, 2, 4, G])
        top_p = sb("top_p", [P, 2, 4, NP3, G], BF16)
        top_t = sb("top_t", [NP3 * G, 2, PT], BF16)
        sums_t = sb("sums_t", [P, 2, PT])
        scaled = sb("scaled", [P, 2, 4, G, VC])
        rden = sb("rden", [P, PB, H])
        o_p = sb("o_p", [P, PB, D])
        o_t = sb("o_t", [P, PT])
        y1 = sb("y1", [P, PB, D])
        y2 = sb("y2", [P, PB, D])
        y3 = sb("y3", [P, PB, D])

        st_ps = ps("st_ps", [P, STBANKS, PT])
        s_ps = ps("s_ps", [P, SBANKS, PT])
        pv_ps = ps("pv_ps", [P, PT])
        mix_ps = ps("mix_ps", [P, PT])
        mixb_ps = mix_ps[:, :].bitcast(BF16)

        def small_bank(kind, p):
            ahead = isinstance(p, int) and p < AHEAD
            return pv_ps if ahead and (kind == "k" or (kind == "xt" and p == 1)) else mix_ps

        for name in """waited x_loaded0 x_loaded1 x_loaded2 x_loaded3 biases_loaded weights_loaded wr_loaded
                wrep_loaded
                stats_done mean_done norm_ready sqrt_done setup_dve
                pool_const rows_set wbd_ready wf_scaled wf_full wf_ready
                rstd_ready weights_used xn_ready xt_full xt_copied qk_full qk_hi qk_float qk_res qk_mid qk_low
                split_stored
                v_full v_done v_copied vt_full scanned carry_done suf_full suf_done
                xs_done half_done fine_done pos_done neg_done far_done xq_done xdq_done
                ffn_full z_done th_done sig_done gate_done
                upper_loaded0 upper_loaded1 lower_loaded0 lower_loaded1 s_full diag_copied diag_masked
                diag_reduced s_reduced
                top_ready negated e0_ready hi_ready res_ready mid_ready low_ready rows_full rows_copied rows_loaded
                v_op_zero v_op_ready st_full exp_done masked pv_done sums_copied sums_full scaled_done num_done
                den_inverted o_done ot_full ot_copied y_full y1_done y2_done y3_done stored""".split():
            sem(name)
        S = sems

        block = ctx.enter_context(nc.Block())

        def wait_apart(engine, semaphore, value):
            engine.wait_ge(semaphore, value)
            engine.sem_inc(S["waited"], 1)

        def piece_block(p):
            return 8 * (p // 2) + 4 * (1 - p % 2)

        def piece_carry(p):
            return p + p // 2

        def parts(p):
            if isinstance(p, int) and p == 1:
                return probs[:, 0:NP3, :].bitcast(BF16).rearrange("p c (s t) -> p s c t", s=2)
            return qk_p[:, :, :, :]

        def turned(p):
            return probs[:, NP3, :] if isinstance(p, int) and p == 1 else xn_t

        def products(engine, stage, p):
            if stage == "times":
                mine = num[:, bass.ds(piece_block(p), PB), :, :]
                if later(p):
                    engine.wait_ge(S["ot_full"], p)
                engine.wait_ge(S["den_inverted"], p + 1)
                engine.tensor_tensor(o_p[:, :, :].rearrange("p n (h e) -> p n h e", e=HE), mine[:, :, :, 0:HE],
                                     rden[:, :, :].rearrange("p n (h a) -> p n h a", a=1)
                                     .to_broadcast([P, PB, H, HE]), ALU.mult).then_inc(S["o_done"], 1)
            elif stage == "add":
                blk = piece_block(p)
                engine.wait_ge(S["y1_done"], p + 1)
                engine.wait_ge(S["gate_done"], p + 1)
                if later(p):
                    engine.wait_ge(S["y3_done"], p)
                engine.tensor_tensor(y2[:, :, :], y1[:, :, :], gate[:, bass.ds(blk, PB), :], ALU.mult)\
                    .then_inc(S["y2_done"], 1)
                engine.wait_ge(S["y2_done"], p + 1)
                if later(p):
                    engine.wait_ge(S["stored"], 16 * p)
                engine.tensor_tensor(y3[:, :, :], y2[:, :, :], x_all[:, bass.ds(blk, PB), :], ALU.add)\
                    .then_inc(S["y3_done"], 1)

        def step_batch(u):
            return u // 2

        def step_head(u, par):
            return 8 * (u % 2) + 4 * par

        def run(engine, do):
            def pair(u):
                for event in events(u):
                    do(*event)
            for event in events_ahead():
                do(*event)
            for u in range(AHEAD):
                pair(u)
            with engine.Fori(AHEAD, PAIRS - AHEAD) as u:
                pair(u)
            for u in range(PAIRS - AHEAD, PAIRS):
                pair(u)
            for event in events_left():
                do(*event)

        @block.sync
        def _(sp):
            x_v = x.rearrange("b (n p) d -> p (b n) d", p=P)
            sp.dma_start(x_all[:, 0:CB, :], x_v[:, 0:CB, :]).then_inc(S["x_loaded0"], 16)
            sp.dma_start(wrep[:, :], wqkv.rearrange("(a e) f -> a e f", a=1).to_broadcast([H, HE, 3 * HE]))\
                .then_inc(S["wrep_loaded"], 16)
            for b in range(1, B):
                sp.dma_start(x_all[:, CB * b:CB * (b + 1), :], x_v[:, CB * b:CB * (b + 1), :])\
                    .then_inc(S[f"x_loaded{b}"], 16)

            def store_split(p, heads=slice(0, H)):
                tok = P * piece_block(p)
                lanes = slice(HE * heads.start, HE * heads.stop)
                for side in range(2):
                    wait_apart(sp, S["qk_low"], 2 * p + side + 1)
                    for c in range(NP3):
                        rows = split_dram[0, heads, :, :, c, bass.ds(tok, PT)] if side == 0 else \
                            split_dram[1, heads, :, c, :, bass.ds(tok, PT)]
                        sp.dma_start(rows.rearrange("h f c t -> (h f) c t"), parts(p)[lanes, side, :, :])\
                            .then_inc(S["split_stored"], 16)

            def first_operands():
                for p in range(AHEAD):
                    store_split(p, slice(0, G))
                    sp.wait_ge(S["split_stored"], SPLIT * (p + 1))
                    load_operands(1 - p, 0, 0)
                for p in range(AHEAD):
                    store_split(p, slice(G, H))
                sp.wait_ge(S["split_stored"], SPLIT * 2 * AHEAD)
                for half in (1, 0):
                    load_operands(half, 0, 1)

            def load_operands(half, u, par):
                if later(u):
                    wait_apart(sp, S["split_stored"], SPLIT * (AHEAD + pieces_for(u)))
                    t = 2 * (u - 1) + par
                    wait_apart(sp, S["st_full"], NAU * t + (AHALF1 if half else NAU))
                    wait_apart(sp, S["s_full"], NSU * (t + 1))
                tok, head = C * step_batch(u) + PT * half, step_head(u, par)
                done = S[f"upper_loaded{par}"] if half else S[f"lower_loaded{par}"]
                for side, op in enumerate((q_op, k_op)):
                    rows = split_dram[side, bass.ds(head, G), :, :, :, bass.ds(tok, PT)]
                    sp.dma_start(op[0:ROWS, par, :, half * PT:(half + 1) * PT],
                                 rows.rearrange("h f a b t -> (f a b) h t")).then_inc(done, 16)

            def load_rows(par, half, t):
                sp.wait_ge(S["rows_copied"], 2 * t + (1 if half else 2))
                sp.dma_start(q_op[MROW:MROW + NP3, par, :, half * PT:(half + 1) * PT], top_t[:, half, :])\
                    .then_inc(S["rows_loaded"], 16)

            out_v = out.rearrange("b (n p) d -> p (b n) d", p=P)

            def store_out(p):
                wait_apart(sp, S["y3_done"], p + 1)
                sp.dma_start(out_v[:, bass.ds(piece_block(p), PB), :], y3[:, :, :]).then_inc(S["stored"], 16)

            def do(what, u, par, of):
                if what == "READ" and of[0] == "rows":
                    load_rows(par, of[1], 2 * u + par)
                elif what == "PREPARE" and of[0] == "split" and later(u, AHEAD):
                    store_split(u)
                elif what == "FINISH" and of[0] == "add":
                    store_out(u)
                elif what == "LOAD":
                    load_operands(of[0], u, par)

            sp.wait_ge(S["rows_set"], 3)
            first_operands()
            run(sp, do)
            sp.wait_ge(S["stored"], 16 * PIECES)

        @block.scalar
        def _(act):
            for dst, src in (
                (bqk[:, 0:1], bqkv[0:HE].rearrange("(a e f) -> a e f", a=1, f=1).to_broadcast([H, HE, 1])),
                (bqk[:, 1:2], bqkv[HE:2 * HE].rearrange("(a e f) -> a e f", a=1, f=1).to_broadcast([H, HE, 1])),
            ):
                act.dma_start(dst, src).then_inc(S["biases_loaded"], 16)

            def statistics(c):
                act.wait_ge(S["norm_ready"], c + 1)
                blocks = slice(0, CB) if c == 0 else slice(CB, NBLK)
                act.activation(std[:, blocks], vareps[:, blocks], ACT.Sqrt).then_inc(S["sqrt_done"], 1)

            def prepare(stage, p):
                if stage == "read xt":
                    act.wait_ge(S["xt_full"], p + 1)
                    if later(p, AHEAD):
                        act.wait_ge(S["v_full"], p)
                        act.wait_ge(S["scanned"], p)
                        act.wait_ge(S["xs_done"], p)
                    act.activation(turned(p)[:, :], small_bank("xt", p)[:, :], ACT.Copy).then_inc(S["xt_copied"], 1)
                elif stage in ("read q", "read k"):
                    side = int(stage == "read k")
                    act.wait_ge(S["qk_full"], 2 * p + side + 1)
                    if later(p, AHEAD):
                        act.wait_ge(S["split_stored"], SPLIT * (AHEAD + p))
                    act.activation(parts(p)[:, side, 0, :], small_bank("qk"[side], p)[:, :], ACT.Identity,
                                   bias=bqk[:, side:side + 1]).then_inc(S["qk_hi"], 1)
                    if later(p):
                        act.wait_ge(S["qk_res"], 2 * p + side - 1)
                    act.activation(qk_f[:, side, :], small_bank("qk"[side], p)[:, :], ACT.Identity,
                                   bias=bqk[:, side:side + 1]).then_inc(S["qk_float"], 1)
                elif stage == "scale":
                    if later(p):
                        act.wait_ge(S["fine_done"], p)
                        act.wait_ge(S["neg_done"], p)
                    act.activation(xs[:, :], turned(p)[:, :], ACT.Copy, scale=risc[:, 0:1])\
                        .then_inc(S["xs_done"], 1)
                    act.wait_ge(S["xs_done"], p + 1)
                    act.activation(xs_half[:, :], xs[:, :], ACT.Copy, scale=0.5).then_inc(S["half_done"], 1)
                elif stage == "rescale":
                    act.wait_ge(S["xq_done"], p + 1)
                    if later(p):
                        act.wait_ge(S["ffn_full"], p)
                    act.activation(x_dq[:, :], x_q[:, :], ACT.Copy, scale=isc[:, 0:1]).then_inc(S["xdq_done"], 1)
                elif stage == "keep v":
                    act.wait_ge(S["v_done"], p + 1)
                    act.activation(v_all[:, bass.ds(piece_block(p), PB), :, 0:HE],
                                   v_p[:, :, :].rearrange("p n (h e) -> p n h e", e=HE), ACT.Copy)\
                        .then_inc(S["v_copied"], 1)
                elif stage == "read suf":
                    act.wait_ge(S["suf_full"], p + 1)
                    act.activation(num[:, bass.ds(piece_block(p), PB), :, 0:HE],
                                   mix_ps[:, :].rearrange("p (n h e) -> p n h e", n=PB, e=HE), ACT.Copy)\
                        .then_inc(S["suf_done"], 1)
                elif stage == "tanh":
                    act.wait_ge(S["z_done"], p + 1)
                    if later(p):
                        act.wait_ge(S["gate_done"], p)
                    act.activation(th[:, :, :], z[:, :, :], ACT.Tanh, scale=0.5).then_inc(S["th_done"], 1)

            def diag_copy(n, t):
                k = sum(v[0] for v in SU[:n])
                act.wait_ge(S["s_full"], NSU * t + n + 1)
                if k >= 4 or later(t):
                    act.wait_ge(S["diag_reduced"], 4 * t + k // 2 - 1)
                act.activation(diag[:, k // 2 % 2, k % 2, :, :],
                               s_ps[:, n % SBANKS, :].rearrange("p (h k) -> p h k", h=G), ACT.Copy)\
                    .then_inc(S["diag_copied"], 1)

            def weights0(half, par, t):
                act.wait_ge(S["top_ready"], 2 * t + (1 if half else 2))
                act.activation(e0[:, par, half, :, :], top[:, half, :, :], ACT.Exp, scale=-SCALE)\
                    .then_inc(S["e0_ready"], 1)

            def rows_copy(half, t):
                act.wait_ge(S["rows_full"], 2 * t + (1 if half else 2))
                if later(t):
                    act.wait_ge(S["rows_loaded"], 16 * (2 * t - (1 if half else 0)))
                act.activation(top_t[:, half, :], mixb_ps[0:NP3 * G, 0:PT], ACT.Copy)\
                    .then_inc(S["rows_copied"], 1)

            def exps(n, t):
                half, kb, heads, q0, nq = AU[n]
                act.wait_ge(S["st_full"], NAU * t + n + 1)
                m, back = slot_before(n, RING, NAU)
                if later(t, back):
                    act.wait_ge(S["pv_done"], NPV * (t - back) + PV_OF[m] + 1)
                w = len(heads) * nq
                act.activation(probs[:, n % RING, 0:w], st_ps[:, n % STBANKS, 0:w], ACT.Exp, scale=SCALE)\
                    .then_inc(S["exp_done"], 1)

            def copy_sums(half, t):
                act.wait_ge(S["pv_done"], NPV * t + (NPV1 if half else NPV))
                if later(t):
                    act.wait_ge(S["sums_full"], 2 * t - (1 if half else 0))
                act.activation(sums_t[:, half, :], pv_ps[:, :], ACT.Copy).then_inc(S["sums_copied"], 1)

            def finish(stage, p):
                if stage == "read ot":
                    act.wait_ge(S["ot_full"], p + 1)
                    act.activation(o_t[:, :], mix_ps[:, :], ACT.Copy).then_inc(S["ot_copied"], 1)

            def do(what, u, par, of):
                if what == "AU":
                    exps(of[0], 2 * u + par)
                elif what == "SU" and SU[of[0]][0]:
                    diag_copy(of[0], 2 * u + par)
                elif what == "WEIGHT":
                    weights0(of[0], par, 2 * u + par)
                elif what == "READ" and of[0] == "rows":
                    rows_copy(of[1], 2 * u + par)
                elif what == "SUMS":
                    copy_sums(of[0], 2 * u + par)
                elif what == "SETUP" and of[0] == "statistics":
                    statistics(u)
                elif what == "SETUP" and of[0] == "weights":
                    act.wait_ge(S["weights_used"], 2)
                    act.wait_ge(S["wf_full"], 1)
                    act.activation(wf_t[:, :], mix_ps[:, 0:P], ACT.Copy).then_inc(S["wf_ready"], 1)
                elif what == "PREPARE":
                    prepare(of[0], u)
                elif what == "FINISH":
                    finish(of[0], u)

            statistics(0)
            for dst, src in (
                (bv[:, :], bqkv[2 * HE:].rearrange("(a b e) -> a b e", a=1, b=1).to_broadcast([P, H, HE])),
                (wf_raw[:, :], wffn),
                (wsc[:, :], wscale.rearrange("(a d) -> a d", a=1).to_broadcast([P, 1])),
                (isc[:, :], iscale.rearrange("(a d) -> a d", a=1).to_broadcast([P, 1])),
                (bf_sb[:, :], bffn.rearrange("(a d) -> a d", a=1).to_broadcast([P, D])),
            ):
                act.dma_start(dst, src).then_inc(S["weights_loaded"], 16)
            for dst, src in (
                (wr_sb[:, :], wr),
                (br_sb[:, :], br.rearrange("(a d) -> a d", a=1).to_broadcast([P, D])),
            ):
                act.dma_start(dst, src).then_inc(S["wr_loaded"], 16)
            act.wait_ge(S["biases_loaded"], 32)
            run(act, do)

        @block.tensor
        def _(pe):
            pe.wait_ge(S["pool_const"], 3)
            pe.wait_ge(S["wbd_ready"], 6)

            def quarters(product, done, bank=mix_ps):
                for i in range(PB):
                    mm = product(bank[:, P * i:P * (i + 1)], i)
                mm.then_inc(S[done], 1)

            def times(w, operand):
                return lambda to, i: pe.matmul(to, operand[:, P * i:P * (i + 1)], w, start=True, stop=True)

            def fill(kind, n, t=None):
                if kind == "xt":
                    pe.wait_ge(S["xn_ready"], PB * n + PB)
                    quarters(lambda to, i: pe.transpose(to, xn[:, i, :], ident[:, :]), "xt_full",
                             small_bank(kind, n))
                    return S["xt_copied"], n + 1
                if kind in ("q", "k"):
                    side = int(kind == "k")
                    pe.wait_ge(S["xt_copied"], n + 1)
                    pe.matmul(small_bank(kind, n)[:, :], wbd[:, side, :], turned(n)[:, :], start=True, stop=True)\
                        .then_inc(S["qk_full"], 1)
                    return S["qk_float"], 2 * n + side + 1
                if kind == "v":
                    quarters(times(wbd[:, 2, :], turned(n)), "v_full")
                    return S["v_done"], n + 1
                if kind == "vt":
                    pe.wait_ge(S["v_done"], n + 1)
                    quarters(lambda to, i: pe.transpose(to, v_p[:, i, :], ident[:, :]), "vt_full")
                    return S["scanned"], n + 1
                if kind == "suf":
                    pe.wait_ge(S["scanned"], n + 1)
                    quarters(lambda to, i: pe.transpose(to, suf_t[:, P * i:P * (i + 1)], ident[:, :]), "suf_full")
                    return S["suf_done"], n + 1
                if kind == "ffn":
                    pe.wait_ge(S["xdq_done"], n + 1)
                    quarters(times(wf_t[:, :], x_dq), "ffn_full")
                    return S["z_done"], n + 1
                if kind == "ot":
                    pe.wait_ge(S["o_done"], n + 1)
                    quarters(lambda to, i: pe.transpose(to, o_p[:, i, :], ident[:, :]), "ot_full")
                    return S["ot_copied"], n + 1
                if kind == "y":
                    pe.wait_ge(S["ot_copied"], n + 1)
                    quarters(times(wr_sb[:, :], o_t), "y_full")
                    return S["y1_done"], n + 1
                if kind == "rows":
                    half = n
                    pe.wait_ge(S["low_ready"], 2 * t + (1 if half else 2))
                    for i in range(4):
                        mm = pe.transpose(mixb_ps[0:NP3 * G, P * i:P * (i + 1)], top_p[:, half, i, :, :],
                                          identb[:, :])
                    mm.then_inc(S["rows_full"], 1)
                    return S["rows_copied"], 2 * t + (1 if half else 2)
                half = n
                pe.wait_ge(S["sums_copied"], 2 * t + (1 if half else 2))
                quarters(lambda to, i: pe.transpose(to, sums_t[:, half, P * i:P * (i + 1)], ident[:, :]), "sums_full")
                return S["num_done"], 2 * t + (1 if half else 2)

            def scores(n, u, par):
                t = 2 * u + par
                is_diag, i, heads, k0, nk = SU[n]
                if n == 0:
                    pe.wait_ge(S[f"upper_loaded{par}"], 32 * (u + 1))
                if n == LOWER:
                    pe.wait_ge(S[f"lower_loaded{par}"], 32 * (u + 1))
                m, back = slot_before(n, SBANKS, NSU)
                if later(t, back):
                    before = sum(v[0] == SU[m][0] for v in SU[:m]) + 1
                    if SU[m][0]:
                        pe.wait_ge(S["diag_copied"], NSD * (t - back) + before)
                    else:
                        pe.wait_ge(S["s_reduced"], NSR * (t - back) + before)
                w = nk * P
                for c, h in enumerate(heads):
                    mm = pe.matmul(s_ps[:, n % SBANKS, c * w:(c + 1) * w], q_op[0:MROW, par, h, P * i:P * (i + 1)],
                                   k_op[0:MROW, par, h, P * k0:P * (k0 + nk)], start=True, stop=True)
                mm.then_inc(S["s_full"], 1)

            def attend(n, u, par):
                t = 2 * u + par
                half, kb, heads, q0, nq = AU[n]
                m, back = slot_before(n, STBANKS, NAU)
                if later(t, back):
                    pe.wait_ge(S["exp_done"], NAU * (t - back) + m + 1)
                if n == 0 or AU[n - 1][0] != half:
                    pe.wait_ge(S["rows_loaded"], 32 * t + (16 if half else 32))
                for c, h in enumerate(heads):
                    mm = pe.matmul(st_ps[:, n % STBANKS, c * nq:(c + 1) * nq],
                                   k_op[:, par, h, P * kb:P * (kb + 1)], q_op[:, par, h, q0:q0 + nq],
                                   start=True, stop=True)
                mm.then_inc(S["st_full"], 1)

            def values(m, u, par):
                t = 2 * u + par
                half, kb = PV[m]
                pe.wait_ge(S["exp_done"], NAU * t + PV_UNITS[m][-1] + 1)
                if PV_UNITS[m][-1] in MASKED:
                    pe.wait_ge(S["masked"], NMASK * t + MASKED.index(PV_UNITS[m][-1]) + 1)
                if m == 0:
                    pe.wait_ge(S["v_op_ready"], t + 1)
                if m in (0, NPV1) and later(t, half):
                    pe.wait_ge(S["sums_copied"], 2 * t + (0 if half else 1))
                for n in PV_UNITS[m]:
                    _, _, heads, q0, nq = AU[n]
                    for c, h in enumerate(heads):
                        mm = pe.matmul(pv_ps[32 * h:32 * (h + 1), q0 - half * PT:q0 - half * PT + nq],
                                       v_op[:, par, kb, h, :], probs[:, n % RING, c * nq:(c + 1) * nq],
                                       start=(m in (0, NPV1)), stop=(m + 1 in (NPV1, NPV)), skip_group_check=True)
                mm.then_inc(S["pv_done"], 1)

            read = [None]

            def refill(kind, n, t=None):
                if isinstance(n, int) and small_bank(kind, n) is pv_ps:
                    if kind == "k" and n == 0:
                        pe.wait_ge(S["xt_copied"], 2)
                    elif kind == "k":
                        pe.wait_ge(S["qk_float"], 2)
                    fill(kind, n, t)
                    return
                if read[0]:
                    pe.wait_ge(*read[0])
                read[0] = fill(kind, n, t)

            def do(what, u, par, of):
                if what == "AU":
                    if of[0] == 0 and par == 0 and later(u):
                        read[0] = (S["num_done"], 4 * u - 1)
                    attend(of[0], u, par)
                elif what == "PV":
                    values(of[0], u, par)
                elif what == "SU":
                    scores(of[0], u, par)
                elif what == "FILL":
                    refill(of[0], of[1], 2 * u + par)
                elif what in ("PREPARE", "FINISH") and of[0].startswith("fill"):
                    refill(of[0].split()[1], u)
                elif what == "SETUP" and of[0] == "weights":
                    pe.wait_ge(*read[0])
                    pe.wait_ge(S["wf_scaled"], 1)
                    pe.wait_ge(S["wr_loaded"], 32)
                    pe.transpose(mix_ps[:, 0:P], wf_dq[:, :], ident[:, :]).then_inc(S["wf_full"], 1)
                    read[0] = S["wf_ready"], 1

            run(pe, do)

        @block.vector
        def _(dve):
            dve.memset(v_all[:, :, :, HE:VC], 1.0).then_inc(S["setup_dve"], 1)
            dve.memset(carry[:, :], 0.0).then_inc(S["setup_dve"], 1)
            dve.memset(tops[:, :, :, :, :], 0.0).then_inc(S["setup_dve"], 1)

            def measure(b):
                dve.wait_ge(S[f"x_loaded{b}"], 16)
                for n in range(CB * b, CB * (b + 1)):
                    dve.bn_stats(stats[:, n, :], x_all[:, n, :]).then_inc(S["stats_done"], 1)

            def statistics(c):
                first, end = (0, CB) if c == 0 else (CB, NBLK)
                dve.wait_ge(S["stats_done"], end)
                b = slice(first, end)
                dve.tensor_tensor(mean2[:, b], stats[:, b, 1], stats[:, b, 4], ALU.add).then_inc(S["mean_done"], 1)
                dve.tensor_tensor(dev[:, b], stats[:, b, 1], stats[:, b, 4], ALU.subtract)\
                    .then_inc(S["mean_done"], 1)
                dve.tensor_tensor(m2[:, b], stats[:, b, 2], stats[:, b, 5], ALU.add).then_inc(S["mean_done"], 1)
                dve.wait_ge(S["mean_done"], 6 * c + 3)
                dve.tensor_scalar(mean[:, b], mean2[:, b], 0.5, None, ALU.mult).then_inc(S["mean_done"], 1)
                dve.tensor_tensor(dev2[:, b], dev[:, b], dev[:, b], ALU.mult).then_inc(S["mean_done"], 1)
                dve.wait_ge(S["mean_done"], 6 * c + 5)
                dve.scalar_tensor_tensor(out=var[:, b], in0=dev2[:, b], scalar=D / 4.0, in1=m2[:, b],
                                         op0=ALU.mult, op1=ALU.add).then_inc(S["mean_done"], 1)
                dve.wait_ge(S["mean_done"], 6 * c + 6)
                dve.tensor_scalar(vareps[:, b], var[:, b], 1.0 / D, EPS, ALU.mult, ALU.add)\
                    .then_inc(S["norm_ready"], 1)
                dve.wait_ge(S["sqrt_done"], c + 1)
                dve.reciprocal(rstd[:, b], std[:, b]).then_inc(S["rstd_ready"], 1)

            def weights():
                dve.wait_ge(S["wr_loaded"], 32)
                dve.wait_ge(S["weights_loaded"], 80)
                dve.tensor_scalar(wf_dq[:, :], wf_raw[:, :], wsc[:, 0:1], None, ALU.mult)\
                    .then_inc(S["wf_scaled"], 1)
                dve.reciprocal(risc[:, :], isc[:, :]).then_inc(S["weights_used"], 1)
                dve.wait_ge(S["pool_const"], 4)
                dve.tensor_copy(count[:, :], count_i[:, :]).then_inc(S["weights_used"], 1)
                dve.wait_ge(S["weights_used"], 2)
                for b in range(B):
                    dve.tensor_copy(num[:, CB * b:CB * (b + 1), :, HE],
                                    count[:, :].rearrange("p (n a) -> p n a", a=1).to_broadcast([P, CB, H]))\
                        .then_inc(S["setup_dve"], 1)

            def prepare(stage, p):
                if stage == "norm":
                    blk = piece_block(p)
                    dve.wait_ge(S["rstd_ready"], 2 if later(p, AHEAD) else 1)
                    if later(p):
                        dve.wait_ge(S["xt_full"], p)
                    for i in range(PB):
                        dve.tensor_scalar(xn[:, i, :], x_all[:, bass.ds(blk + i, 1), :],
                                          mean[:, bass.ds(blk + i, 1)], rstd[:, bass.ds(blk + i, 1)],
                                          ALU.subtract, ALU.mult).then_inc(S["xn_ready"], 1)
                elif stage in ("mid q", "mid k") and not later(p, AHEAD):
                    side = int(stage == "mid k")
                    n = 2 * p + side + 1
                    dve.wait_ge(S["qk_float"], n)
                    dve.tensor_tensor(parts(p)[:, side, 1, :], qk_f[:, side, :], parts(p)[:, side, 0, :],
                                      ALU.subtract).then_inc(S["qk_mid"], 1)
                    if later(p):
                        dve.wait_ge(S["qk_low"], n - 2)
                    dve.tensor_tensor(qk_r[:, side, :], qk_f[:, side, :], parts(p)[:, side, 0, :],
                                      ALU.subtract).then_inc(S["qk_res"], 1)
                elif stage == "read v":
                    dve.wait_ge(S["v_full"], p + 1)
                    if later(p):
                        dve.wait_ge(S["v_copied"], p)
                    dve.tensor_tensor(v_p[:, :, :], mix_ps[:, :].rearrange("p (n d) -> p n d", n=PB),
                                      bv[:, :].rearrange("p (a d) -> p a d", a=1).to_broadcast([P, PB, D]), ALU.add)\
                        .then_inc(S["v_done"], 1)
                elif stage == "read vt":
                    dve.wait_ge(S["vt_full"], p + 1)
                    if later(p):
                        dve.wait_ge(S["suf_full"], p)
                        dve.wait_ge(S["carry_done"], p)
                    else:
                        dve.wait_ge(S["setup_dve"], 3 + B)
                    dve.tensor_tensor_scan(suf_t[:, ::-1], mix_ps[:, ::-1], turned(p)[:, :],
                                           carry[:, bass.ds(piece_carry(p), 1)], ALU.add, ALU.bypass)\
                        .then_inc(S["scanned"], 1)
                    dve.wait_ge(S["scanned"], p + 1)
                    dve.tensor_copy(carry[:, bass.ds(piece_carry(p) + 1, 1)],
                                    suf_t[:, 0:1]).then_inc(S["carry_done"], 1)
                elif stage == "near":
                    wait_apart(dve, S["half_done"], p + 1)
                    if later(p):
                        wait_apart(dve, S["far_done"], p)
                        wait_apart(dve, S["xq_done"], p)
                    dve.tensor_scalar(x_fine[:, :], xs[:, :], FINE, -FINE, ALU.min, ALU.max, saturate=False)\
                        .then_inc(S["fine_done"], 1)
                    dve.tensor_scalar(x_pos[:, :], xs_half[:, :], FINE / 2, FP8_MAX / 2, ALU.max, ALU.min,
                                      saturate=False).then_inc(S["pos_done"], 1)
                    dve.tensor_scalar(x_neg[:, :], xs_half[:, :], -FINE / 2, -FP8_MAX / 2, ALU.min, ALU.max,
                                      saturate=False).then_inc(S["neg_done"], 1)
                elif stage == "far":
                    wait_apart(dve, S["neg_done"], p + 1)
                    wait_apart(dve, S["pos_done"], p + 1)
                    dve.tensor_tensor(x_far[:, :], x_pos[:, :], x_neg[:, :], ALU.add).then_inc(S["far_done"], 1)
                    wait_apart(dve, S["far_done"], p + 1)
                    wait_apart(dve, S["fine_done"], p + 1)
                    dve.scalar_tensor_tensor(out=x_q[:, :], in0=x_far[:, :], scalar=2.0, in1=x_fine[:, :],
                                             op0=ALU.mult, op1=ALU.add).then_inc(S["xq_done"], 1)
                elif stage == "read ffn":
                    dve.wait_ge(S["ffn_full"], p + 1)
                    if later(p):
                        dve.wait_ge(S["gate_done"], p)
                    dve.tensor_tensor(z[:, :, :], mix_ps[:, :].rearrange("p (n d) -> p n d", n=PB),
                                      bf_sb[:, :].rearrange("p (a d) -> p a d", a=1).to_broadcast([P, PB, D]),
                                      ALU.add).then_inc(S["z_done"], 1)
                elif stage == "gate":
                    dve.wait_ge(S["th_done"], p + 1)
                    dve.tensor_scalar(th[:, :, :], th[:, :, :], 0.5, 0.5, ALU.mult, ALU.add)\
                        .then_inc(S["sig_done"], 1)

            def finish(stage, p):
                if stage == "divide":
                    ended = 2 * STEPS - (PIECES - 1 - p) if later_than_loop(p) else 4 * (p + AHEAD)
                    dve.wait_ge(S["num_done"], ended)
                    if later(p):
                        dve.wait_ge(S["o_done"], p)
                    dve.reciprocal(rden[:, :, :], num[:, bass.ds(piece_block(p), PB), :, HE])\
                        .then_inc(S["den_inverted"], 1)
                elif stage == "read y":
                    dve.wait_ge(S["y_full"], p + 1)
                    if later(p):
                        dve.wait_ge(S["y2_done"], p)
                    dve.tensor_tensor(y1[:, :, :], mix_ps[:, :].rearrange("p (n d) -> p n d", n=PB),
                                      br_sb[:, :].rearrange("p (a d) -> p a d", a=1).to_broadcast([P, PB, D]),
                                      ALU.add).then_inc(S["y1_done"], 1)

                elif later_than_loop(p):
                    products(dve, stage, p)

            def reduce(n, t):
                is_diag, i, heads, k0, nk = SU[n]
                half = i // 4
                if is_diag:
                    return
                r = n - sum(v[0] for v in SU[:n])
                dve.wait_ge(S["s_full"], NSU * t + n + 1)
                slot = 0 if k0 == 0 else 1
                dve.tensor_reduce(tops[:, half, i % 4, heads[0]:heads[-1] + 1, slot],
                                  s_ps[:, n % SBANKS, 0:len(heads) * nk * P].rearrange("p (h k) -> p h k", h=len(heads)),
                                  AX.X, ALU.max).then_inc(S["s_reduced"], 1)

            def reduce_diag(k, t):
                half, i = (1, 0) if k < 2 else (0, 0)
                i = 2 * (k % 2)
                dve.wait_ge(S["diag_masked"], 4 * t + k + 1)
                dve.tensor_reduce(tops[:, half, i:i + 2, :, 2],
                                  diag[:, k % 2, :, :, :], AX.X, ALU.max).then_inc(S["diag_reduced"], 1)

            def maxima(half, t):
                n = 2 * t + (1 if half else 2)
                dve.wait_ge(S["s_reduced"], NSR * t + (HALF1_R if half else NSR))
                dve.wait_ge(S["diag_reduced"], 4 * t + (2 if half else 4))
                if later(t):
                    dve.wait_ge(S["e0_ready"], n - 2)
                    dve.wait_ge(S["low_ready"], n - 2)
                dve.tensor_reduce(top[:, half, :, :], tops[:, half, :, :, :], AX.X, ALU.max)\
                    .then_inc(S["top_ready"], 1)

            def gather(half, u, par):
                t = 2 * u + par
                n = 2 * t + (1 if half else 2)
                mine = num[:, bass.ds(CB * step_batch(u) + 4 * half, 4), bass.ds(step_head(u, par), G), :]
                dve.wait_ge(S["e0_ready"], n)
                dve.wait_ge(S["suf_done"], pieces_for(u))
                if later(t):
                    dve.wait_ge(S["num_done"], n - 2)
                dve.tensor_tensor(scaled[:, half, :, :, :], mine,
                                  e0[:, par, half, :, :].rearrange("p i (h a) -> p i h a", a=1)
                                  .to_broadcast([P, 4, G, VC]), ALU.mult).then_inc(S["scaled_done"], 1)
                dve.wait_ge(S["sums_full"], n)
                dve.wait_ge(S["scaled_done"], n)
                dve.tensor_tensor(mine, scaled[:, half, :, :, :],
                                  mix_ps[:, :].rearrange("p (i h c) -> p i h c", i=4, h=G)[:, :, :, 0:VC],
                                  ALU.add).then_inc(S["num_done"], 1)

            def do(what, u, par, of):
                if what == "SU":
                    reduce(of[0], 2 * u + par)
                    if of[0] in DIAG_AFTER:
                        reduce_diag(DIAG_AFTER[of[0]], 2 * u + par)
                elif what == "MAX":
                    maxima(of[0], 2 * u + par)
                elif what == "READ" and of[0] == "out":
                    gather(of[1], u, par)
                elif what == "SETUP" and of[0] == "measure":
                    measure(u)
                elif what == "SETUP" and of[0] == "statistics":
                    statistics(u)
                elif what == "SETUP" and of[0] == "weights":
                    weights()
                elif what == "PREPARE":
                    prepare(of[0], u)
                elif what == "FINISH":
                    finish(of[0], u)

            measure(0)
            statistics(0)
            run(dve, do)

        @block.gpsimd
        def _(pool):
            pool.memset(ident[:, :], 0.0).then_inc(S["pool_const"], 1)
            pool.wait_ge(S["pool_const"], 1)
            pool.affine_select(out=ident[:, :], in_=ident[:, :], compare_op=ALU.not_equal, fill=1.0, base=0,
                               pattern=[[-1, P]], channel_multiplier=1).then_inc(S["pool_const"], 1)
            pool.wait_ge(S["pool_const"], 2)
            pool.tensor_copy(identb[:, :], ident[:, :]).then_inc(S["pool_const"], 1)
            pool.iota(count_i[:, :], pattern=[[-P, CB]], base=C, channel_multiplier=-1)\
                .then_inc(S["pool_const"], 1)
            pool.wait_ge(S["wrep_loaded"], 16)
            for m in range(3):
                src = wrep[:, HE * m:HE * (m + 1)].rearrange("p (a f) -> p a f", a=1).to_broadcast([P, H, HE])
                pool.affine_select(out=wbd_half[:, m, :].rearrange("p (h f) -> p h f", h=H), in_=src,
                                   compare_op=ALU.is_ge, fill=0.0, base=0, pattern=[[-HE, H], [0, HE]],
                                   channel_multiplier=1).then_inc(S["wbd_ready"], 1)
            pool.wait_ge(S["wbd_ready"], 3)
            for m in range(3):
                pool.affine_select(out=wbd[:, m, :].rearrange("p (h f) -> p h f", h=H),
                                   in_=wbd_half[:, m, :].rearrange("p (h f) -> p h f", h=H),
                                   compare_op=ALU.is_ge, fill=0.0, base=HE - 1,
                                   pattern=[[HE, H], [0, HE]], channel_multiplier=-1).then_inc(S["wbd_ready"], 1)
            pool.wait_ge(S["wbd_ready"], 6)
            pool.memset(q_op[64:128, :, :, :].bitcast(F32), 0.0).then_inc(S["rows_set"], 1)
            pool.wait_ge(S["rows_set"], 1)
            pool.memset(k_op[64:128, :, :, :].bitcast(F32), 0.0).then_inc(S["rows_set"], 1)
            pool.wait_ge(S["rows_set"], 2)
            pool.memset(k_op[MROW:MROW + NP3, :, :, :].bitcast(F32), TWO_ONES).then_inc(S["rows_set"], 1)
            pool.wait_ge(S["rows_set"], 3)
            pool.wait_ge(S["wbd_ready"], 6)

            def prepare(stage, p):
                side = int(stage[-1] == "k")
                n = 2 * p + side + 1
                if stage[:-2] == "mid" and later(p, AHEAD):
                    pool.wait_ge(S["qk_float"], n)
                    pool.tensor_tensor(qk_p[:, side, 1, :], qk_f[:, side, :], qk_p[:, side, 0, :], ALU.subtract)\
                        .then_inc(S["qk_mid"], 1)
                    pool.wait_ge(S["qk_low"], n - 2)
                    pool.tensor_tensor(qk_r[:, side, :], qk_f[:, side, :], qk_p[:, side, 0, :], ALU.subtract)\
                        .then_inc(S["qk_res"], 1)
                elif stage[:-2] == "low":
                    pool.wait_ge(S["qk_mid"], n)
                    pool.wait_ge(S["qk_res"], n)
                    pool.tensor_tensor(parts(p)[:, side, 2, :], qk_r[:, side, :], parts(p)[:, side, 1, :],
                                       ALU.subtract).then_inc(S["qk_low"], 1)
                elif stage == "gate":
                    pool.wait_ge(S["sig_done"], p + 1)
                    pool.tensor_tensor(gate[:, bass.ds(piece_block(p), PB), :], z[:, :, :], th[:, :, :], ALU.mult)\
                        .then_inc(S["gate_done"], 1)

            def finish(stage, p):
                if not later_than_loop(p):
                    products(pool, stage, p)

            def mask_diag(k, t):
                wait_apart(pool, S["diag_copied"], NSD * t + 2 * k + 2)
                tile = diag[:, k % 2, :, :, :].rearrange("p i h k -> p (i h) k")
                pool.affine_select(out=tile, in_=tile, compare_op=ALU.is_gt, fill=0.0, base=0,
                                   pattern=[[0, 2 * G], [-1, P]], channel_multiplier=1)\
                    .then_inc(S["diag_masked"], 1)

            def max_parts(half, t):
                n = 2 * t + (1 if half else 2)
                hi, mid, low = (top_p[:, half, :, c, :] for c in range(NP3))
                if later(t):
                    pool.wait_ge(S["rows_full"], n - 2)
                wait_apart(pool, S["top_ready"], n)
                pool.tensor_scalar(top_n[:, half, :, :], top[:, half, :, :], -1.0, None, ALU.mult)\
                    .then_inc(S["negated"], 1)
                pool.tensor_scalar(hi, top[:, half, :, :], -1.0, None, ALU.mult).then_inc(S["hi_ready"], 1)
                pool.wait_ge(S["negated"], n)
                pool.wait_ge(S["hi_ready"], n)
                pool.tensor_tensor(mid, top_n[:, half, :, :], hi, ALU.subtract).then_inc(S["mid_ready"], 1)
                pool.tensor_tensor(top_r[:, half, :, :], top_n[:, half, :, :], hi, ALU.subtract)\
                    .then_inc(S["res_ready"], 1)
                pool.wait_ge(S["mid_ready"], n)
                pool.wait_ge(S["res_ready"], n)
                pool.tensor_tensor(low, top_r[:, half, :, :], mid, ALU.subtract).then_inc(S["low_ready"], 1)

            def load_v(u, par):
                t = 2 * u + par
                if later(t, 2):
                    pool.wait_ge(S["pv_done"], NPV * (t - 1))
                elif t == 0:
                    pool.memset(v_op[:, :, :, :, :], 0.0).then_inc(S["v_op_zero"], 1)
                    pool.wait_ge(S["v_op_zero"], 1)
                    pool.wait_ge(S["setup_dve"], 1)
                pool.wait_ge(S["v_copied"], pieces_for(u))
                pool.tensor_copy(v_op[:, par, :, :, 0:VC],
                                 v_all[:, bass.ds(CB * step_batch(u), CB), bass.ds(step_head(u, par), G), :])\
                    .then_inc(S["v_op_ready"], 1)

            def mask_exps(n, t):
                half, kb, heads, q0, nq = AU[n]
                wait_apart(pool, S["exp_done"], NAU * t + n + 1)
                tile = probs[:, n % RING, 0:len(heads) * nq].rearrange("p (h q) -> p h q", q=nq)[:, :, 0:P]
                pool.affine_select(out=tile, in_=tile, compare_op=ALU.is_gt, fill=0.0, base=0,
                                   pattern=[[0, len(heads)], [1, P]], channel_multiplier=-1)\
                    .then_inc(S["masked"], 1)

            def do(what, u, par, of):
                if what == "AU" and of[0] in MASKED:
                    mask_exps(of[0], 2 * u + par)
                elif what == "SU" and of[0] in MASK_AFTER:
                    mask_diag(MASK_AFTER[of[0]], 2 * u + par)
                elif what == "PARTS":
                    max_parts(of[0], 2 * u + par)
                elif what == "LOADV":
                    load_v(u, par)
                elif what == "PREPARE":
                    prepare(of[0], u)
                elif what == "FINISH":
                    finish(of[0], u)

            run(pool, do)


_INS = ["L0_attn_x", "L0_attn_Wqkv", "L0_attn_bqkv", "L0_attn_Wr", "L0_attn_br", "L0_ffn_weight_fp8",
        "L0_ffn_bias", "L0_ffn_input_scale", "L0_ffn_weight_scale"]


def kernel(**inputs):
    import concourse.bacc as bacc
    from concourse.bass_utils import run_bass_kernel_spmd

    nc = bacc.Bacc("TRN2", target_bir_lowering=False, num_devices=1)
    arrays, args = {}, []
    for name in _INS:
        a = np.ascontiguousarray(inputs[name])
        arrays[name] = a
        args.append(nc.dram_tensor(name, a.shape, mybir.dt.from_np(a.dtype), kind="ExternalInput").ap())
    args.append(nc.dram_tensor("out", (B, C, D), F32, kind="ExternalOutput").ap())
    program(nc, *args)
    r = run_bass_kernel_spmd(nc, [arrays], core_ids=[0])
    return r.results[0]["out"]
```
